# Optimizing a Trainium2 kernel written in Bass

```python
import numpy as np
import jax
import jax.numpy as jnp

def _softmax(x, axis=-1):
    return jax.nn.softmax(x, axis=axis)

def _gelu(x):
    return jax.nn.gelu(x, approximate=True)

def _silu(x):
    return jax.nn.silu(x)

def _sigmoid(x):
    return jax.nn.sigmoid(x)

def _layernorm(x, axis=-1, eps=1e-05):
    m = jnp.mean(x, axis=axis, keepdims=True)
    v = jnp.var(x, axis=axis, keepdims=True)
    return (x - m) / jnp.sqrt(v + eps)

def _scatter_add(tgt, idx, src, axis=0):
    return tgt.at[idx].add(src)

def _segment_sum(src, seg, n):
    return jax.ops.segment_sum(src, seg, n)
kernel_name = 'mk_decoder_postln_d2_seqx_r8_0a8ebe'

def setup_inputs(seed: int=0):
    np.random.seed(seed)
    _w = jnp.asarray

    def _rec_inputs():
        import jax
        import jax.numpy as jnp
        _rk = jax.random.key(seed)
        x = -0.000125 + 0.9999 * jax.random.normal(jax.random.fold_in(_rk, 1), (8, 128, 256), jnp.float32)
        _lenS = 128 - jax.random.randint(jax.random.fold_in(_rk, 7), (8,), 0, max(1, 128 // 4) + 1, jnp.int32)
        _lenS2 = 128 - jax.random.randint(jax.random.fold_in(_rk, 8), (8,), 0, max(1, 128 // 4) + 1, jnp.int32)
        _ctx_2048P = jax.random.normal(jax.random.fold_in(_rk, 11), (8, 16, 256), jnp.float32)
        _ctx_2048c = jax.random.dirichlet(jax.random.fold_in(_rk, 511), 0.3 * jnp.ones((16,), jnp.float32), (8, 128))
        _ctx_2048t = jnp.einsum('bsk,bkd->bsd', _ctx_2048c, _ctx_2048P)
        _ctx_2048t = _ctx_2048t * jax.lax.rsqrt(jnp.mean(jnp.square(_ctx_2048t)) + 1e-12) * 0.953939
        ctx_2048 = -1.52775e-05 + 0.999936 * (_ctx_2048t + 0.3 * jax.random.normal(jax.random.fold_in(_rk, 611), (8, 128, 256), jnp.float32))
        return (x, ctx_2048)
    x, ctx_2048 = _rec_inputs()

    def _L0_attn_setup():
        import jax, jax.numpy as jnp
        import numpy as np
        EMBED_DIM = 256
        NUM_HEADS = 16
        HEAD_DIM = EMBED_DIM // NUM_HEADS
        B, T = (2, 256)
        key = jax.random.key(seed)
        ks = jax.random.split(key, 5)
        s = 1.0 / np.sqrt(EMBED_DIM)
        return {'x': jax.random.normal(ks[0], (B, T, EMBED_DIM), dtype=jnp.float32), 'Wq': jax.random.uniform(ks[1], (EMBED_DIM, EMBED_DIM), jnp.float32, -s, s), 'Wk': jax.random.uniform(ks[2], (EMBED_DIM, EMBED_DIM), jnp.float32, -s, s), 'Wv': jax.random.uniform(ks[3], (EMBED_DIM, EMBED_DIM), jnp.float32, -s, s), 'Wo': jax.random.uniform(ks[4], (EMBED_DIM, EMBED_DIM), jnp.float32, -s, s)}
    _L0_attn_all = _L0_attn_setup()
    _L0_attn_in = {k: v for k, v in _L0_attn_all.items() if k in ('Wq', 'Wk', 'Wv', 'Wo')}
    del _L0_attn_all

    def _L0_xattn_setup():
        import jax, jax.numpy as jnp
        import numpy as np
        B, DIM1, DIM2, LATENT, T = (16, 128, 128, 64, 256)
        LN_EPS = 1e-05
        key = jax.random.key(seed)
        ks = jax.random.split(key, 8)

        def xavier(k, shape):
            fan_out, fan_in = shape
            std = float(np.sqrt(2.0 / (fan_in + fan_out)))
            return jax.random.normal(k, shape, dtype=jnp.float32) * std
        return {'input1': jax.random.normal(ks[0], (B, DIM1, T), dtype=jnp.float32), 'input2': jax.random.normal(ks[1], (B, DIM2, T), dtype=jnp.float32), 'theta_w': xavier(ks[2], (LATENT, DIM2)), 'theta_b': jnp.zeros((LATENT,), jnp.float32), 'phi_w': xavier(ks[3], (LATENT, DIM1)), 'phi_b': jnp.zeros((LATENT,), jnp.float32), 'g_w': xavier(ks[4], (LATENT, DIM1)), 'g_b': jnp.zeros((LATENT,), jnp.float32), 'ln_gamma': jnp.ones((LATENT, T), jnp.float32), 'ln_beta': jnp.zeros((LATENT, T), jnp.float32), 'out_w': xavier(ks[5], (DIM2, LATENT)), 'out_b': jnp.zeros((DIM2,), jnp.float32)}
    _L0_xattn_all = _L0_xattn_setup()
    _L0_xattn_in = {k: v for k, v in _L0_xattn_all.items() if k in ('theta_w', 'theta_b', 'phi_w', 'phi_b', 'g_w', 'g_b', 'ln_gamma', 'ln_beta', 'out_w', 'out_b')}
    del _L0_xattn_all

    def _L0_ffn_setup():
        import jax, jax.numpy as jnp
        import numpy as np
        BLOCK = 64

        def dequant4bit(q, scale):
            return (q.astype(jnp.float32) - 7.5) * jnp.repeat(scale, BLOCK, axis=1)
        key = jax.random.key(seed)
        ks = jax.random.split(key, 11)
        B, S, D, H, R = (4, 256, 256, 1024, 16)
        return {'x1': jax.random.normal(ks[0], (B, S, D), jnp.float32), 'w_up_q': jax.random.randint(ks[1], (H, D), 0, 16, dtype=jnp.int32), 'w_up_scale': jax.random.uniform(ks[2], (H, D // BLOCK), jnp.float32) * 0.02, 'b_up': jax.random.normal(ks[3], (H,), jnp.float32) * 0.01, 'w_up_lora_a': jax.random.normal(ks[4], (D, R), jnp.float32) * 0.02, 'w_up_lora_b': jax.random.normal(ks[5], (R, H), jnp.float32) * 0.02, 'w_down_q': jax.random.randint(ks[6], (D, H), 0, 16, dtype=jnp.int32), 'w_down_scale': jax.random.uniform(ks[7], (D, H // BLOCK), jnp.float32) * 0.02, 'b_down': jax.random.normal(ks[8], (D,), jnp.float32) * 0.01, 'w_down_lora_a': jax.random.normal(ks[9], (H, R), jnp.float32) * 0.02, 'w_down_lora_b': jax.random.normal(ks[10], (R, D), jnp.float32) * 0.02}
    _L0_ffn_all = _L0_ffn_setup()
    _L0_ffn_in = {k: v for k, v in _L0_ffn_all.items() if k in ('w_up_q', 'w_up_scale', 'b_up', 'w_up_lora_a', 'w_up_lora_b', 'w_down_q', 'w_down_scale', 'b_down', 'w_down_lora_a', 'w_down_lora_b')}
    del _L0_ffn_all

    def _L1_attn_setup():
        import jax, jax.numpy as jnp
        import numpy as np
        B, S, H_DIM = (2, 256, 256)
        N_HEADS, D_HEAD = (16, 128)
        key = jax.random.key(seed)
        k1, k2, k3 = jax.random.split(key, 3)
        x = jax.random.normal(k1, (B, S, H_DIM), dtype=jnp.float32)
        w_qkv = jax.random.normal(k2, (H_DIM, 3 * N_HEADS * D_HEAD), dtype=jnp.float32) * 0.02
        w_o = jax.random.normal(k3, (N_HEADS * D_HEAD, H_DIM), dtype=jnp.float32) * 0.02
        return {'x': x, 'w_qkv': w_qkv, 'w_o': w_o}
    _L1_attn_all = _L1_attn_setup()
    _L1_attn_in = {k: v for k, v in _L1_attn_all.items() if k in ('w_qkv', 'w_o')}
    del _L1_attn_all

    def _L1_xattn_setup():
        import jax, jax.numpy as jnp
        import numpy as np
        N_HEAD = 8
        key = jax.random.key(seed)
        k1, k2, k3 = jax.random.split(key, 3)
        b, d, m = (4, 128, 256)
        c, n = (128, 256)
        q = jax.random.normal(k1, (b, d, m), dtype=jnp.float32)
        k = jax.random.normal(k2, (d // d * b, d, n), dtype=jnp.float32).reshape(b, d, n)
        v = jax.random.normal(k3, (b, c, n), dtype=jnp.float32)
        return {'q': q, 'k': k, 'v': v}
    _L1_xattn_all = _L1_xattn_setup()
    _L1_xattn_in = {k: v for k, v in _L1_xattn_all.items() if k in ()}
    del _L1_xattn_all

    def _L1_ffn_setup():
        import jax, jax.numpy as jnp
        import numpy as np
        NUM_EXPERTS = 64
        TOP_K = 8
        HIDDEN = 256
        INTER = 128
        key = jax.random.key(seed)
        k1, k2, k3, k4 = jax.random.split(key, 4)
        scale = 1.0 / np.sqrt(HIDDEN)
        hidden_states = jax.random.normal(k1, (4, 256, HIDDEN), dtype=jnp.float32)
        gate_w = jax.random.normal(k2, (NUM_EXPERTS, HIDDEN), dtype=jnp.float32) * scale
        w13 = jax.random.normal(k3, (NUM_EXPERTS, 2 * INTER, HIDDEN), dtype=jnp.float32) * scale
        w2 = jax.random.normal(k4, (NUM_EXPERTS, HIDDEN, INTER), dtype=jnp.float32) * (1.0 / np.sqrt(INTER))
        return {'hidden_states': hidden_states, 'gate_w': gate_w, 'w13': w13, 'w2': w2}
    _L1_ffn_all = _L1_ffn_setup()
    _L1_ffn_in = {k: v for k, v in _L1_ffn_all.items() if k in ('gate_w', 'w13', 'w2')}
    del _L1_ffn_all
    return {'x': x, 'ctx_2048': ctx_2048, 'L0_attn_Wq': _L0_attn_in['Wq'], 'L0_attn_Wk': _L0_attn_in['Wk'], 'L0_attn_Wv': _L0_attn_in['Wv'], 'L0_attn_Wo': _L0_attn_in['Wo'], 'L0_xattn_theta_w': _L0_xattn_in['theta_w'], 'L0_xattn_theta_b': _L0_xattn_in['theta_b'], 'L0_xattn_phi_w': _L0_xattn_in['phi_w'], 'L0_xattn_phi_b': _L0_xattn_in['phi_b'], 'L0_xattn_g_w': _L0_xattn_in['g_w'], 'L0_xattn_g_b': _L0_xattn_in['g_b'], 'L0_xattn_ln_gamma': _L0_xattn_in['ln_gamma'], 'L0_xattn_ln_beta': _L0_xattn_in['ln_beta'], 'L0_xattn_out_w': _L0_xattn_in['out_w'], 'L0_xattn_out_b': _L0_xattn_in['out_b'], 'L0_ffn_w_up_q': _L0_ffn_in['w_up_q'], 'L0_ffn_w_up_scale': _L0_ffn_in['w_up_scale'], 'L0_ffn_b_up': _L0_ffn_in['b_up'], 'L0_ffn_w_up_lora_a': _L0_ffn_in['w_up_lora_a'], 'L0_ffn_w_up_lora_b': _L0_ffn_in['w_up_lora_b'], 'L0_ffn_w_down_q': _L0_ffn_in['w_down_q'], 'L0_ffn_w_down_scale': _L0_ffn_in['w_down_scale'], 'L0_ffn_b_down': _L0_ffn_in['b_down'], 'L0_ffn_w_down_lora_a': _L0_ffn_in['w_down_lora_a'], 'L0_ffn_w_down_lora_b': _L0_ffn_in['w_down_lora_b'], 'L1_attn_w_qkv': _L1_attn_in['w_qkv'], 'L1_attn_w_o': _L1_attn_in['w_o'], 'L1_ffn_gate_w': _L1_ffn_in['gate_w'], 'L1_ffn_w13': _L1_ffn_in['w13'], 'L1_ffn_w2': _L1_ffn_in['w2']}

def reference(x, ctx_2048, L0_attn_Wq, L0_attn_Wk, L0_attn_Wv, L0_attn_Wo, L0_xattn_theta_w, L0_xattn_theta_b, L0_xattn_phi_w, L0_xattn_phi_b, L0_xattn_g_w, L0_xattn_g_b, L0_xattn_ln_gamma, L0_xattn_ln_beta, L0_xattn_out_w, L0_xattn_out_b, L0_ffn_w_up_q, L0_ffn_w_up_scale, L0_ffn_b_up, L0_ffn_w_up_lora_a, L0_ffn_w_up_lora_b, L0_ffn_w_down_q, L0_ffn_w_down_scale, L0_ffn_b_down, L0_ffn_w_down_lora_a, L0_ffn_w_down_lora_b, L1_attn_w_qkv, L1_attn_w_o, L1_ffn_gate_w, L1_ffn_w13, L1_ffn_w2):
    import jax
    import jax.numpy as jnp

    def _L0_attn_ref(x, Wq, Wk, Wv, Wo):
        import jax, jax.numpy as jnp
        import numpy as np
        EMBED_DIM = 256
        NUM_HEADS = 16
        HEAD_DIM = EMBED_DIM // NUM_HEADS
        B, T = (2, 256)
        Bsz, Tlen, C = x.shape
        H, D = (NUM_HEADS, HEAD_DIM)

        def proj(W):
            return (x @ W.T).reshape(Bsz, Tlen, H, D).transpose(0, 2, 1, 3)
        q, k, v = (proj(Wq), proj(Wk), proj(Wv))
        att = jnp.einsum('bhqd,bhkd->bhqk', q, k) / jnp.sqrt(jnp.float32(D))
        causal = jnp.tril(jnp.ones((Tlen, Tlen), dtype=bool))
        att = jnp.where(causal, att, -jnp.inf)
        att = jax.nn.softmax(att, axis=-1)
        out = jnp.einsum('bhqk,bhkd->bhqd', att, v)
        out = out.transpose(0, 2, 1, 3).reshape(Bsz, Tlen, C)
        return out @ Wo.T

    def _L0_xattn_ref(input1, input2, theta_w, theta_b, phi_w, phi_b, g_w, g_b, ln_gamma, ln_beta, out_w, out_b):
        import jax, jax.numpy as jnp
        import numpy as np
        B, DIM1, DIM2, LATENT, T = (16, 128, 128, 64, 256)
        LN_EPS = 1e-05
        theta_x = jnp.einsum('ld,bdt->btl', theta_w, input2) + theta_b
        phi_x = jnp.einsum('ld,bdt->blt', phi_w, input1) + phi_b[:, None]
        scores = jnp.einsum('btl,bls->bts', theta_x, phi_x)
        p = jax.nn.softmax(scores, axis=-1)
        g_x = jnp.einsum('ld,bdt->btl', g_w, input1) + g_b
        t_x = jnp.einsum('bts,bsl->blt', p, g_x)
        mu = jnp.mean(t_x, axis=(1, 2), keepdims=True)
        var = jnp.var(t_x, axis=(1, 2), keepdims=True)
        h = (t_x - mu) * jax.lax.rsqrt(var + LN_EPS) * ln_gamma + ln_beta
        h = jax.nn.relu(h)
        w_t = jnp.einsum('ol,blt->bot', out_w, h) + out_b[None, :, None]
        return w_t + input2

    def _L0_ffn_ref(x1, w_up_q, w_up_scale, b_up, w_up_lora_a, w_up_lora_b, w_down_q, w_down_scale, b_down, w_down_lora_a, w_down_lora_b):
        import jax, jax.numpy as jnp
        import numpy as np
        BLOCK = 64

        def dequant4bit(q, scale):
            return (q.astype(jnp.float32) - 7.5) * jnp.repeat(scale, BLOCK, axis=1)
        w_up = dequant4bit(w_up_q, w_up_scale).T
        y1 = x1 @ w_up + b_up + x1 @ w_up_lora_a @ w_up_lora_b
        x2 = jax.nn.relu(y1)
        w_down = dequant4bit(w_down_q, w_down_scale).T
        y2 = x2 @ w_down + b_down + x2 @ w_down_lora_a @ w_down_lora_b
        return y2

    def _L1_attn_ref(x, w_qkv, w_o):
        import jax, jax.numpy as jnp
        import numpy as np
        B, S, H_DIM = (2, 256, 256)
        N_HEADS, D_HEAD = (16, 128)
        b, s, _ = x.shape
        qkv = jnp.einsum('bsh,hf->bsf', x, w_qkv)
        qkv = qkv.reshape(b, s, 3, N_HEADS, D_HEAD)
        q, k, v = (qkv[:, :, 0], qkv[:, :, 1], qkv[:, :, 2])
        q = q.transpose(0, 2, 1, 3)
        k = k.transpose(0, 2, 1, 3)
        v = v.transpose(0, 2, 1, 3)
        scores = jnp.einsum('bhqd,bhkd->bhqk', q, k) / jnp.sqrt(jnp.float32(D_HEAD))
        probs = jax.nn.softmax(scores, axis=-1)
        values = jnp.einsum('bhqk,bhkd->bhkd', probs, v)
        values = values.transpose(0, 2, 1, 3).reshape(b, s, N_HEADS * D_HEAD)
        out = jnp.einsum('bsf,fh->bsh', values, w_o)
        return out

    def _L1_xattn_ref(q, k, v):
        import jax, jax.numpy as jnp
        import numpy as np
        N_HEAD = 8
        b, d, m = q.shape
        c = v.shape[1]
        h = N_HEAD
        qh = q.reshape(b * h, d // h, m)
        kh = k.reshape(b * h, d // h, -1)
        vh = v.reshape(b * h, c // h, -1)
        scale = 1.0 / jnp.sqrt(jnp.asarray(d // h, dtype=q.dtype))
        qk = jnp.einsum('bdm,bdn->bmn', qh, kh) * scale
        sm = jax.nn.softmax(qk, axis=-1)
        ret = jnp.einsum('bmn,bcn->bcm', sm, vh)
        return ret.reshape(b, c, m)

    def _L1_ffn_ref(hidden_states, gate_w, w13, w2):
        import jax, jax.numpy as jnp
        import numpy as np
        NUM_EXPERTS = 64
        TOP_K = 8
        HIDDEN = 256
        INTER = 128
        orig_shape = hidden_states.shape
        x = hidden_states.reshape(-1, HIDDEN)
        logits = jnp.einsum('th,eh->te', x, gate_w)
        probs = jax.nn.softmax(logits, axis=-1)
        topk_w, topk_idx = jax.lax.top_k(probs, TOP_K)
        combine = (jax.nn.one_hot(topk_idx, NUM_EXPERTS, dtype=x.dtype) * topk_w[..., None]).sum(axis=1)

        def step(acc, inp):
            w13_e, w2_e, c = inp
            g = x @ w13_e[:INTER].T
            u = x @ w13_e[INTER:].T
            h = jax.nn.silu(g) * u
            o = h @ w2_e.T
            return (acc + c[:, None] * o, None)
        out0 = jnp.zeros_like(x)
        out, _ = jax.lax.scan(step, out0, (w13, w2, combine.T))
        return out.reshape(orig_shape)
    x = _layernorm(x + _L0_attn_ref(x, L0_attn_Wq, L0_attn_Wk, L0_attn_Wv, L0_attn_Wo), axis=-1)
    x = _layernorm(x + _L0_xattn_ref(x, ctx_2048, L0_xattn_theta_w, L0_xattn_theta_b, L0_xattn_phi_w, L0_xattn_phi_b, L0_xattn_g_w, L0_xattn_g_b, L0_xattn_ln_gamma, L0_xattn_ln_beta, L0_xattn_out_w, L0_xattn_out_b), axis=-1)
    x = _layernorm(x + _L0_ffn_ref(x, L0_ffn_w_up_q, L0_ffn_w_up_scale, L0_ffn_b_up, L0_ffn_w_up_lora_a, L0_ffn_w_up_lora_b, L0_ffn_w_down_q, L0_ffn_w_down_scale, L0_ffn_b_down, L0_ffn_w_down_lora_a, L0_ffn_w_down_lora_b), axis=-1)
    x = _layernorm(x + _L1_attn_ref(x, L1_attn_w_qkv, L1_attn_w_o), axis=-1)
    x = _layernorm(x + _L1_xattn_ref(x, ctx_2048, ctx_2048), axis=-1)
    x = _layernorm(x + _L1_ffn_ref(x, L1_ffn_gate_w, L1_ffn_w13, L1_ffn_w2), axis=-1)
    return x

_drawn_inputs = setup_inputs


def setup_inputs(seed=0):
    import zlib

    import numpy as np

    out = dict(_drawn_inputs(seed))
    spreads = {'L0_xattn_theta_b': (0.0, 0.1),
     'L0_xattn_phi_b': (0.0, 0.8),
     'L0_xattn_g_b': (0.0, 0.312),
     'L0_xattn_ln_gamma': (1.0, 0.2),
     'L0_xattn_ln_beta': (0.0, 0.1),
     'L0_xattn_out_b': (0.0, 0.8)}
    factors = {'L0_ffn_b_up': 5.502,
     'L0_ffn_w_up_lora_a': 2.817,
     'L0_ffn_w_up_lora_b': 2.767,
     'L0_ffn_b_down': 5.041}
    for name, (base, spread) in spreads.items():
        noise = np.random.default_rng([zlib.crc32(name.encode()), seed]).standard_normal(out[name].shape)
        drawn = base * np.exp(spread * noise) if base else spread * noise
        out[name] = jnp.asarray(drawn.astype(out[name].dtype))
    for name, factor in factors.items():
        out[name] = (out[name] * factor).astype(out[name].dtype)
    return out
```

```python
from contextlib import ExitStack

import numpy as np

import concourse.bass as bass
from concourse import mybir

F32 = mybir.dt.float32
BF16 = mybir.dt.bfloat16
I32 = mybir.dt.int32
U32 = mybir.dt.uint32
ALU = mybir.AluOpType
ACT = mybir.ActivationFunctionType
AX = mybir.AxisListType

P = 128
NSEQ = 8
D = 256
KD = D // P
TOK = NSEQ * P
LANES = 2
EPS = 1e-5

H0, HD0 = 16, 16
HP = P // HD0
LAT = 64
FF, FT = 1024, 8
QBLK, RANK = 64, 16
H1, HD1 = 16, 128
HX, HDX = 8, 16
NE, TOPK, INTER = 64, 8, 128
ROWS = TOK
NT = 128
TABLE = NE * ROWS + NT * P
TPT = 8
LAG = 2
PARTS = 4
WCOLS = KD * 2 * INTER + D


class Token:

    def __init__(self, play, name, at):
        self.play, self.name, self.at, self.final = play, name, at, None


class Prev:

    def __init__(self, label):
        self.label = label


class Flow:

    def __init__(self, nc, ctx):
        self.nc, self.ctx = nc, ctx
        self.engines = {"pe": nc.tensor, "act": nc.scalar, "dve": nc.vector, "pool": nc.gpsimd, "sp": nc.sync}
        self.sems, self.total = {}, {}
        self.passed = ctx.enter_context(nc.semaphore("passed"))
        self.plays = 0
        self.begin()

    def begin(self):
        self.plays += 1
        self.steps, self.count, self.labels, self.tokens = [], {}, {}, []

    def latest(self, label):
        return self.labels.get(label) or Prev(label)

    def step(self, engine, after, calls, label=None, stream=None, apart=False):
        name, amount = (stream, 16) if stream else (engine, 1)
        if name not in self.sems:
            self.sems[name] = self.ctx.enter_context(self.nc.semaphore("done_" + name))
            self.total[name] = 0
        self.count[name] = self.count.get(name, 0) + amount
        token = Token(self.plays, name, self.count[name])
        self.tokens.append(token)
        if label:
            self.labels[label] = token
        self.steps.append((engine, list(after), calls, name, amount, apart or engine == "sp"))
        return token

    def pe(self, after, calls, label=None, apart=False):
        return self.step("pe", after, calls, label, apart=apart)

    def act(self, after, call, *args, label=None, **kw):
        return self.step("act", after, [(call, args, kw)], label)

    def dve(self, after, call, *args, label=None, apart=False, **kw):
        return self.step("dve", after, [(call, args, kw)], label, apart=apart)

    def pool(self, after, call, *args, label=None, **kw):
        return self.step("pool", after, [(call, args, kw)], label)

    def dma(self, after, engine, stream, out, in_, label=None):
        return self.step(engine, after, [(self.engines[engine].dma_start, (out, in_), {})], label, stream)

    def play(self, times=1, join=True):
        nc = self.nc
        if join:
            self.join()
        for name, amount in self.count.items():
            if times > 1 and self.total[name] < amount + 1:
                owner = next(s[0] for s in self.steps if s[3] == name)
                if owner == "pool" != name:
                    continue
                more = amount + 16 - amount % 16
                self.engines[owner].sem_inc(self.sems[name], more)
                self.total[name] += more
        base = dict(self.total)

        def value(token, i):
            if isinstance(token, Prev) and times == 1:
                return self.before[token.label].name, self.before[token.label].final, None
            if isinstance(token, Prev):
                t = self.labels[token.label]
                turn, c = self.count[t.name], base[t.name] + t.at - self.count[t.name]
            elif token.play == self.plays:
                t, turn, c = token, self.count[token.name], base[token.name] + token.at
            else:
                return token.name, token.final, None
            return t.name, (c if times == 1 else i * turn + c), c

        def emit(i):
            seen = {}
            for engine, after, calls, name, amount, apart in self.steps:
                eng = self.engines[engine]
                for token in after:
                    sem, v, c = value(token, i)
                    if c is not None:
                        if seen.get((engine, sem), -1) >= c:
                            continue
                        seen[engine, sem] = c
                    eng.wait_ge(self.sems[sem], v)
                    if apart and c is not None and times > 1:
                        eng.sem_inc(self.passed, 1)
                for call, args, kw in calls:
                    args = [a(i) if callable(a) else a for a in args]
                    last = call(*args, **kw)
                last.then_inc(self.sems[name], amount)

        if times == 1:
            emit(0)
        else:
            with nc.Fori(0, times) as i:
                emit(i)
        for t in self.tokens:
            t.final = base[t.name] + (times - 1) * self.count[t.name] + t.at
        for name, amount in self.count.items():
            self.total[name] += times * amount
        self.before = self.labels
        self.begin()

    def join(self):
        for eng in self.engines.values():
            for name, total in self.total.items():
                if total:
                    eng.wait_ge(self.sems[name], total)


def interleave(*lanes):
    lanes = list(lanes)
    while lanes:
        for lane in list(lanes):
            if next(lane, "end") == "end":
                lanes.remove(lane)


def spread(ap, n, axis):
    shape = list(ap.shape)
    return ap.unsqueeze(axis).broadcast_to(shape[:axis] + [n] + shape[axis:])


def decoder(nc, x_in, ctx_in, w0, thw, outw, bias64, bias128, gb, gamma, beta, upq, ups, upa, upb, dnq, dns, bdn, dna,
            dnb, wqkv, wo1, gatew, we, out, debug=None):
    ctx = ExitStack()
    with ctx:
        def sb(name, shape, dt=F32):
            return ctx.enter_context(nc.sbuf_tensor(name, shape, dt))

        f = Flow(nc, ctx)
        pe, act, dve, pool = nc.tensor, nc.scalar, nc.vector, nc.gpsimd
        ps = ctx.enter_context(nc.psum_tensor("ps", [P, 8, 512], F32))

        def mm(out, lhsT, rhs, start=True, stop=True, shared=False):
            return (pe.matmul, (out, lhsT, rhs), dict(start=start, stop=stop, skip_group_check=shared))

        def tr(out, in_):
            return (pe.transpose, (out, in_, ident[:, :]), {})

        id_parts = [nc.dram_tensor(f"id_part{k}", (TABLE, 1), I32).ap() for k in range(PARTS)]
        ids_table = nc.dram_tensor("ids_table", (TABLE, 1), I32).ap()
        x5_rows = nc.dram_tensor("x5_rows", (TOK, D), F32).ap()
        expert_rows = nc.dram_tensor("expert_rows", ((NT + LAG) * P, D), F32).ap()
        tile_expert_dram = nc.dram_tensor("tile_expert_dram", (NT, 1), I32).ap()

        ident = sb("ident", [P, P])
        identb = sb("identb", [P, P], BF16)
        onesb = sb("onesb", [P, P], BF16)
        before = sb("before", [P, P], BF16)
        future = sb("future", [P, 4, P], BF16)
        headmask = sb("headmask", [P, HP])
        power = sb("power", [P, 8])
        mean64 = sb("mean64", [LAT, LAT])

        x_all = sb("x_all", [P, NSEQ, D])
        xT_all = sb("xT_all", [P, KD, TOK])

        def constants():
            g = []
            g.append(f.pool([], pool.memset, ident[:, :], 0.0))
            g.append(f.pool([], pool.memset, onesb[:, :], 1.0))
            g.append(f.pool([], pool.memset, future[:, :, :], 0.0))
            g.append(f.pool([], pool.memset, headmask[:, :], 1.0))
            g.append(f.pool([], pool.memset, power[:, :], -0.5))
            g.append(f.pool([], pool.memset, mean64[:, :], 1.0 / LAT))
            t = f.pool(g, pool.affine_select, out=ident[:, :], in_=ident[:, :], compare_op=ALU.not_equal, fill=1.0,
                       base=0, pattern=[[-1, P]], channel_multiplier=1)
            f.pool([], pool.affine_select, out=before[:, :], in_=onesb[:, :], compare_op=ALU.is_gt, fill=0.0,
                   base=0, pattern=[[1, P]], channel_multiplier=-1)
            f.pool([], pool.affine_select, out=future[:, :, :], in_=future[:, :, :], compare_op=ALU.is_ge, fill=-1e30,
                   base=0, pattern=[[0, 4], [-1, P]], channel_multiplier=1)
            m = f.pool([], pool.affine_select, out=headmask[:, :], in_=headmask[:, :], compare_op=ALU.is_ge, fill=0.0,
                       base=0, pattern=[[-HD0, HP]], channel_multiplier=1)
            f.pool([m], pool.affine_select, out=headmask[:, :], in_=headmask[:, :], compare_op=ALU.is_ge, fill=0.0,
                   base=HD0 - 1, pattern=[[HD0, HP]], channel_multiplier=-1)
            f.dve([t], dve.tensor_copy, identb[:, :], ident[:, :])

        def norm(L, src, dst, after, label=None):
            t = f.dve(after, dve.bn_stats, L["stats"][:, :], src)
            t = f.dve([t], dve.bn_aggr, L["mv"][:, 0:2], L["stats"][:, :], apart=True)
            t = f.dve([t], dve.tensor_scalar, L["mv"][:, 2:3], L["mv"][:, 1:2], EPS, None, ALU.add)
            t = f.pool([t], pool.tensor_tensor, L["mv"][:, 3:4], L["mv"][:, 2:3], power[:, 0:1], ALU.pow)
            return f.dve([t], dve.tensor_scalar, dst, src, L["mv"][:, 0:1], L["mv"][:, 3:4], ALU.subtract, ALU.mult,
                         label=label)

        def layer0():
            c = ExitStack()

            def sb(name, shape, dt=F32):
                return c.enter_context(nc.sbuf_tensor(name, shape, dt))

            w0_sb = sb("w0_sb", [P, 4, KD, D])
            th_sb = sb("th_sb", [P, 3, LAT])
            outw_sb = sb("outw_sb", [LAT, P])
            b64_sb = sb("b64_sb", [LAT, 2])
            b128_sb = sb("b128_sb", [P, 1 + FT])
            gb_sb = sb("gb_sb", [P, LAT])
            gamma_sb = sb("gamma_sb", [LAT, D])
            beta_sb = sb("beta_sb", [LAT, D])
            bdn_sb = sb("bdn_sb", [P, D])
            wup = sb("wup", [P, KD, FF])
            wdn = sb("wdn", [P, FT, D])
            lanes = []
            for n in range(LANES):
                s = lambda name, shape, dt=F32, n=n: sb(f"{name}_{n}", shape, dt)
                lanes.append(dict(
                    n=n, bank=[ps[:, 4 * n + k, :] for k in range(4)],
                    x=s("x", [P, D]), ctx=s("ctx", [P, D]), xT=s("xT", [P, KD, P]), q=s("q", [P, KD, P]),
                    k=s("k", [P, KD, P]), kheads=s("kheads", [P, KD, HP, P]),
                    vheads=s("vheads", [P, KD, HP * (P + HD0)]), soft=s("soft", [P, H0, P]),
                    pT=s("pT", [P, H0, P]), top=s("top", [P, H0]), rsum=s("rsum", [P, H0]),
                    oT=s("oT", [P, KD, P]), res=s("res", [P, D]), x1=s("x1", [P, D]), x2=s("x2", [P, D]),
                    x3=s("x3", [P, D]), x3T=s("x3T", [P, KD, P]), cx=s("cx", [P, D]), theta=s("theta", [LAT, D]), phi=s("phi", [LAT, D]),
                    g=s("g", [P, 2, LAT]), e=s("e", [P, 2, D]), eT=s("eT", [P, 2, D]), h=s("h", [LAT, D]),
                    hs=s("hs", [LAT, 6]), hm=s("hm", [LAT, 8]), up=s("up", [P, FT, P]),
                    stats=s("stats", [P, 6]), mv=s("mv", [P, 4])))

            c2 = ExitStack()
            upq_sb = c2.enter_context(nc.sbuf_tensor("upq_sb", [P, KD, FF], I32))
            ups_sb = c2.enter_context(nc.sbuf_tensor("ups_sb", [P, KD, FF], F32))
            dnq_sb = c2.enter_context(nc.sbuf_tensor("dnq_sb", [P, FT, D], I32))
            dns_sb = c2.enter_context(nc.sbuf_tensor("dns_sb", [P, FT, D], F32))
            upa_sb = c2.enter_context(nc.sbuf_tensor("upa_sb", [RANK, D], F32))
            upb_sb = c2.enter_context(nc.sbuf_tensor("upb_sb", [RANK, FF], F32))
            dna_sb = c2.enter_context(nc.sbuf_tensor("dna_sb", [RANK, FF], F32))
            dnb_sb = c2.enter_context(nc.sbuf_tensor("dnb_sb", [RANK, D], F32))
            zero_ids = c2.enter_context(nc.sbuf_tensor("zero_ids", [P, TABLE // P], I32))

            def load(stream, dst, src, after=()):
                return f.dma(after, "sp", stream, dst, src)

            load("w", w0_sb[:, :, :, :], w0)
            load("w", th_sb[:, :, :], thw)
            load("w", outw_sb[:, :], outw)
            load("w", b64_sb[:, :], bias64)
            load("w", b128_sb[:, :], bias128)
            load("w", gb_sb[:, :], gb.broadcast_to([P, LAT]))
            load("w", gamma_sb[:, :], gamma)
            load("w", beta_sb[:, :], beta)
            tw = load("w", bdn_sb[:, :], bdn.broadcast_to([P, D]))
            load("q", upq_sb[:, :, :], upq)
            load("q", dnq_sb[:, :, :], dnq)
            for k in range(KD):
                for s in range(2):
                    load("q", ups_sb[s * QBLK:(s + 1) * QBLK, k, :], ups[2 * k + s:2 * k + s + 1, :].broadcast_to([QBLK, FF]))
            for k in range(FT):
                for s in range(2):
                    load("q", dns_sb[s * QBLK:(s + 1) * QBLK, k, :], dns[2 * k + s:2 * k + s + 1, :].broadcast_to([QBLK, D]))
            load("q", upa_sb[:, :], upa)
            load("q", upb_sb[:, :], upb)
            load("q", dna_sb[:, :], dna)
            tq = load("q", dnb_sb[:, :], dnb)
            constants()
            tz = f.dve([], dve.memset, zero_ids[:, :], 0)
            for part in id_parts:
                f.dma([tz], "sp", "table", part.rearrange("(p n) o -> p (n o)", p=P), zero_ids[:, :])
            for L in lanes:
                f.dve([], dve.memset, L["vheads"][:, :, :], 0.0)
            for dst, q, s, a, b, n in ((wup, upq_sb, ups_sb, upa_sb, upb_sb, FF), (wdn, dnq_sb, dns_sb, dna_sb, dnb_sb, D)):
                t1 = f.dve([tq], dve.scalar_tensor_tensor, out=dst[:, :, :], in0=q[:, :, :], scalar=7.5,
                           in1=s[:, :, :], op0=ALU.subtract, op1=ALU.mult)
                calls, last = [], None
                width = min(n, 512)
                flat = dst[:, :, :].rearrange("p k n -> p (k n)")
                for j in range(4):
                    calls = []
                    for o in range(0, 512, width):
                        k, c0 = divmod(j * 512 + o, n)
                        calls.append(mm(ps[:, j, o:o + width], a[:, k * P:(k + 1) * P], b[:, c0:c0 + width]))
                    tp = f.pe([tq] + ([last4[j]] if dst is wdn else []), calls)
                    last = f.dve([tp, t1], dve.tensor_tensor, flat[:, j * 512:(j + 1) * 512],
                                 flat[:, j * 512:(j + 1) * 512], ps[:, j, :], ALU.add)
                    if dst is wup:
                        last4 = (last4 if j else []) + [last]
            f.play(join=False)
            c2.close()
            act.preload_act_table(ACT.Exp)

            def sequence(L):
                n, (b0, b1, b2, b3) = L["n"], L["bank"]

                def was(label):
                    return [Prev(f"{label}{n}")]

                x, soft = L["x"], L["soft"]
                t_x = L["got x"]
                t = f.pe([t_x] + was("free0"), [tr(b0[:, k * P:(k + 1) * P], x[:, k * P:(k + 1) * P]) for k in range(KD)])
                txT = f.act([t], act.copy, L["xT"][:, :, :].rearrange("p k t -> p (k t)"), b0[:, 0:D])
                yield
                calls = []
                for which in range(2):
                    for m in range(KD):
                        for k in range(KD):
                            calls.append(mm(b1[:, (which * KD + m) * P:(which * KD + m + 1) * P],
                                            w0_sb[:, which, k, m * P:(m + 1) * P], L["xT"][:, k, :],
                                            start=k == 0, stop=k == KD - 1))
                tqk = f.pe([txT] + was("free1"), calls)
                tv = f.pe(was("free2"), [mm(b2[:, 0:D], L["xT"][:, k, :], w0_sb[:, 2, k, :], start=k == 0, stop=k == KD - 1)
                                         for k in range(KD)])
                tk = f.act([tqk], act.copy, L["k"][:, :, :].rearrange("p k t -> p (k t)"), b1[:, D:2 * D])
                tq = f.act([], act.copy, L["q"][:, :, :].rearrange("p k t -> p (k t)"), b1[:, 0:D])
                tkh = [f.pool([tk], pool.tensor_tensor, L["kheads"][:, m, :, :], spread(L["k"][:, m, :], HP, 1),
                              spread(headmask[:, :], P, 2), ALU.mult) for m in range(KD)]
                tvh = f.dve([tv], dve.tensor_copy,
                            L["vheads"][:, :, :].rearrange("p k (h s) -> p k h s", s=P + HD0)[:, :, :, 0:HD0],
                            b2[:, 0:D].rearrange("p (k h s) -> p k h s", k=KD, h=HP))
                yield
                free = {0: [txT], 1: [tq], 2: [tvh], 3: was("free3")}
                ts = []
                for m in range(KD):
                    for half in range(2):
                        k = 2 * m + half
                        ts.append(f.pe([tq, tkh[m]] + free[k], [
                            mm(L["bank"][k], identb[:, :], future[:, :, :].rearrange("p a b -> p (a b)"), stop=False),
                            mm(L["bank"][k], L["q"][:, m, :], L["kheads"][:, m, 4 * half:4 * half + 4, :].rearrange("p a b -> p (a b)"), start=False)]))
                yield
                tsub = []
                for k in range(4):
                    hs = slice(4 * k, 4 * k + 4)
                    s3 = L["bank"][k].rearrange("p (h t) -> p h t", h=4)
                    t = f.dve([ts[k]], dve.tensor_reduce, L["top"][:, hs], s3, AX.X, ALU.max)
                    tsub.append(f.dve([t], dve.tensor_tensor, soft[:, hs, :], s3, spread(L["top"][:, hs], P, 2), ALU.subtract))
                    if k % 2:
                        yield
                te = [f.act([tsub[2 * k + 1]], act.activation, soft[:, 8 * k:8 * k + 8, :], soft[:, 8 * k:8 * k + 8, :],
                            ACT.Exp, scale=HD0 ** -0.5) for k in range(2)]
                tn = []
                for k in range(2):
                    hs = slice(8 * k, 8 * k + 8)
                    t = f.dve([te[k]], dve.tensor_reduce, L["rsum"][:, hs], soft[:, hs, :], AX.X, ALU.add)
                    t = f.dve([t], dve.reciprocal, L["rsum"][:, hs], L["rsum"][:, hs])
                    tn.append(f.dve([t], dve.tensor_tensor, soft[:, hs, :], soft[:, hs, :], spread(L["rsum"][:, hs], P, 2), ALU.mult))
                    yield
                tp = []
                for k in range(4):
                    t = f.pe([tn[k // 2]], [tr(L["bank"][k][:, h * P:(h + 1) * P], soft[:, 4 * k + h, :]) for h in range(4)])
                    dst = L["pT"][:, 4 * k:4 * k + 4, :].rearrange("p a b -> p (a b)")
                    tp.append(f.act([t], act.copy, dst, L["bank"][k]) if k % 2 else f.dve([t], dve.tensor_copy, dst, L["bank"][k]))
                    if k % 2:
                        yield
                t = f.pe([tp[1], tp[3], tp[2]], [
                    mm(b0[:, m * P:(m + 1) * P], L["vheads"][:, m, h * P:(h + 1) * P], L["pT"][:, m * HP + h, :],
                       start=h == 0, stop=h == HP - 1) for m in range(KD) for h in range(HP)])
                to = f.act([t], act.copy, L["oT"][:, :, :].rearrange("p k t -> p (k t)"), b0[:, 0:D])
                t = f.pe([to], [mm(b1[:, 0:D], L["oT"][:, k, :], w0_sb[:, 3, k, :], start=k == 0, stop=k == KD - 1)
                                for k in range(KD)])
                tr1 = f.dve([t], dve.tensor_tensor, L["res"][:, :], x[:, :], b1[:, 0:D], ALU.add, label=f"x read{n}")
                yield
                t1 = norm(L, L["res"][:, :], L["x1"][:, :], [tr1])
                tcx = f.pool([t1, L["got ctx"]], pool.tensor_tensor, L["cx"][:, :], L["x1"][:, :], L["ctx"][:, :], ALU.add, label=f"ctx added{n}")
                yield
                t = f.pe([t1, to, L["got ctx"]], [mm(b0[0:LAT, 0:D], th_sb[:, 0, :], L["ctx"][:, :]),
                                    mm(b0[0:LAT, D:2 * D], th_sb[:, 1, :], L["x1"][:, :])], label=f"ctx read{n}")
                tth = f.act([t], act.activation, L["theta"][:, :], b0[0:LAT, 0:D], ACT.Identity, bias=b64_sb[:, 0:1])
                tph = f.act([], act.activation, L["phi"][:, :], b0[0:LAT, D:2 * D], ACT.Identity, bias=b64_sb[:, 1:2])
                t = f.pe([tr1], [mm(b1[:, s * LAT:(s + 1) * LAT], L["x1"][:, s * P:(s + 1) * P], th_sb[:, 2, :]) for s in range(2)])
                tg = f.dve([t], dve.tensor_tensor, L["g"][:, :, :], b1[:, 0:2 * LAT].rearrange("p (s l) -> p s l", s=2),
                           spread(gb_sb[:, :], 2, 1), ALU.add)
                t = f.pe([tph, tp[2]], [mm(b2[:, s * D:(s + 1) * D], L["theta"][:, s * P:(s + 1) * P], L["phi"][:, :]) for s in range(2)])
                yield
                s3 = b2.rearrange("p (s t) -> p s t", s=2)
                tm = f.dve([t], dve.tensor_reduce, L["top"][:, 0:2], s3, AX.X, ALU.max, negate=True)
                te = [f.act([tm], act.activation, L["e"][:, s, :], s3[:, s, :], ACT.Exp, bias=L["top"][:, s:s + 1],
                            accum_out=L["rsum"][:, s:s + 1]) for s in range(2)]
                t = f.dve([te[1]], dve.reciprocal, L["rsum"][:, 0:2], L["rsum"][:, 0:2])
                tn = [f.dve([t], dve.tensor_scalar, L["e"][:, s, :], L["e"][:, s, :], L["rsum"][:, s:s + 1], None, ALU.mult)
                      for s in range(2)]
                yield
                t = f.pe([tn[1], tp[3]], [tr(b3[:, (2 * s + u) * P:(2 * s + u + 1) * P], L["e"][:, u, s * P:(s + 1) * P])
                                          for s in range(2) for u in range(2)])
                teT = f.act([t], act.copy, L["eT"][:, :, :].rearrange("p s t -> p (s t)"), b3)
                tt = f.pe([teT, tg, tph], [mm(b0[0:LAT, 0:D], L["g"][:, s, :], L["eT"][:, s, :], start=s == 0, stop=s == 1)
                                           for s in range(2)])
                hm = L["hm"]
                t = f.dve([tt], dve.bn_stats, L["hs"][:, :], b0[0:LAT, 0:D])
                t = f.dve([t], dve.bn_aggr, hm[:, 0:2], L["hs"][:, :], apart=True)
                t = f.dve([t], dve.scalar_tensor_tensor, out=hm[:, 1:2], in0=hm[:, 0:1], scalar=hm[:, 0:1], in1=hm[:, 1:2],
                          op0=ALU.mult, op1=ALU.add)
                yield
                t = f.pe([t, tg], [mm(b1[0:LAT, 0:2], mean64[:, :], hm[:, 0:2])], apart=True)
                t = f.dve([t], dve.tensor_copy, hm[:, 2:4], b1[0:LAT, 0:2])
                t = f.dve([t], dve.scalar_tensor_tensor, out=hm[:, 4:5], in0=hm[:, 2:3], scalar=hm[:, 2:3], in1=hm[:, 3:4],
                          op0=ALU.mult, op1=ALU.subtract)
                tmu = f.dve([t], dve.tensor_scalar, hm[:, 5:6], hm[:, 4:5], -1.0, EPS, ALU.mult, ALU.add)
                tvr = f.pool([tmu], pool.tensor_tensor, hm[:, 6:7], hm[:, 5:6], power[0:LAT, 0:1], ALU.pow)
                th = f.dve([tmu], dve.scalar_tensor_tensor, out=L["h"][:, :], in0=b0[0:LAT, 0:D], scalar=hm[:, 2:3],
                           in1=gamma_sb[:, :], op0=ALU.subtract, op1=ALU.mult)
                t = f.dve([th, tvr], dve.scalar_tensor_tensor, out=L["h"][:, :], in0=L["h"][:, :], scalar=hm[:, 6:7],
                          in1=beta_sb[:, :], op0=ALU.mult, op1=ALU.add)
                t = f.act([t], act.activation, L["h"][:, :], L["h"][:, :], ACT.Relu)
                yield
                t = f.pe([t, te[1]], [mm(b2[:, 0:D], outw_sb[:, :], L["h"][:, :])])
                tr2 = f.dve([t, tcx], dve.scalar_tensor_tensor, out=L["res"][:, :], in0=b2[:, 0:D], scalar=b128_sb[:, 0:1],
                            in1=L["cx"][:, :], op0=ALU.add, op1=ALU.add)
                t2 = norm(L, L["res"][:, :], L["x2"][:, :], [tr2])
                txb = f.pool([t2], pool.tensor_tensor, L["cx"][:, :], L["x2"][:, :], bdn_sb[:, :], ALU.add)
                yield
                t = f.pe([t2, teT], [tr(b3[:, k * P:(k + 1) * P], L["x2"][:, k * P:(k + 1) * P]) for k in range(KD)])
                t = f.act([t], act.copy, L["xT"][:, :, :].rearrange("p k t -> p (k t)"), b3[:, 0:D])
                tu = []
                for j in range(2):
                    tj = f.pe([t, th if j == 0 else tmu], [
                        mm(L["bank"][j][:, m * P:(m + 1) * P], wup[:, k, (4 * j + m) * P:(4 * j + m + 1) * P], L["xT"][:, k, :],
                           start=k == 0, stop=k == KD - 1) for m in range(4) for k in range(KD)])
                    tj = f.dve([tj], dve.tensor_tensor, L["up"][:, 4 * j:4 * j + 4, :],
                               L["bank"][j].rearrange("p (m t) -> p m t", m=4), spread(b128_sb[:, 1 + 4 * j:5 + 4 * j], P, 2), ALU.add)
                    tu.append(f.act([tj], act.activation, L["up"][:, 4 * j:4 * j + 4, :], L["up"][:, 4 * j:4 * j + 4, :], ACT.Relu,
                                    label=f"free{j}{n}"))
                    yield
                t = f.pe([tu[1], tr2], [mm(b2[:, 0:D], L["up"][:, m, :], wdn[:, m, :], start=m == 0, stop=m == FT - 1)
                                        for m in range(FT)])
                t = f.dve([t, txb], dve.tensor_tensor, L["res"][:, :], b2[:, 0:D], L["cx"][:, :], ALU.add, label=f"free2{n}")
                t = norm(L, L["res"][:, :], L["x3"][:, :], [t] + was("out"))
                f.dma([t], "act", f"out{n}", lambda i: x_all[:, bass.ds(LANES * i + n, 1), :], L["x3"][:, :].unsqueeze(1), label=f"out{n}")
                yield
                t = f.pe([t], [tr(b3[:, k * P:(k + 1) * P], L["x3"][:, k * P:(k + 1) * P]) for k in range(KD)])
                t = f.act([t] + was("outT"), act.copy, L["x3T"][:, :, :].rearrange("p k t -> p (k t)"), b3[:, 0:D], label=f"free3{n}")
                f.dma([t], "act", f"outT{n}", lambda i: xT_all[:, :, bass.ds((LANES * i + n) * P, P)], L["x3T"][:, :, :], label=f"outT{n}")

            for name, src, readers in (("x", x_in, ["x read"]), ("ctx", ctx_in, ["ctx added", "ctx read"])):
                for L in lanes:
                    n = L["n"]
                    L["got " + name] = f.dma([Prev(f"{r}{n}") for r in readers], "sp", f"{name}{n}", L[name][:, :],
                                             lambda i, n=n, src=src: src[LANES * i + n, :, :])
            interleave(*[sequence(L) for L in lanes])
            f.play(NSEQ // LANES)
            c.close()

        layer0()
        def dump(name, src):
            if debug is not None and name in debug:
                f.dma([], "sp", "dbg", debug[name], src)
                f.play()
                f.join()

        dump("x3T", xT_all[:, :, :])

        def attention1():
            c = ExitStack()

            def sb(name, shape, dt=F32):
                return c.enter_context(nc.sbuf_tensor(name, shape, dt))

            wh = sb("wh", [P, KD, 3, HD1])
            wo = sb("wo", [P, D])
            qT, kT = sb("qT1", [P, TOK]), sb("kT1", [P, TOK])
            vT, sums, oT = sb("vT1", [P, TOK]), sb("sums1", [P, TOK]), sb("oT1", [P, TOK])
            soft, rows = sb("soft1", [P, NSEQ, P]), sb("rows1", [P, NSEQ, P])
            top, rsum = sb("top1", [P, NSEQ]), sb("rsum1", [P, NSEQ])
            stats, mv = sb("stats1", [P, NSEQ, 6]), sb("mv1", [P, NSEQ, 2])
            var, rstd = sb("var1", [P, NSEQ]), sb("rstd1", [P, NSEQ])
            y = [ps[:, b // 2, (b % 2) * D:(b % 2 + 1) * D] for b in range(NSEQ)]
            sbank, abank = [ps[:, 4, :], ps[:, 5, :]], [ps[:, 6, :], ps[:, 7, :]]

            def load_qkv(after, head):
                return f.dma(after, "sp", "wh", wh[:, :, :, :], head)

            def project(which, got, read, free):
                name, dst = ("q", "k", "v")[which], (qT, kT, vT)[which]
                done = []
                for half in range(2):
                    cols = slice(half * 512, half * 512 + 512)
                    t = f.pe([got] + free[half], [
                        mm(abank[half], wh[:, k, which, :], xT_all[:, k, cols], start=k == 0, stop=k == KD - 1) for k in range(KD)],
                        label=f"{name} project{half}")
                    done.append(f.act([t] + read, act.copy, dst[:, cols], abank[half], label=f"{name}{half}") if half else
                                f.dve([t] + read, dve.tensor_copy, dst[:, cols], abank[half], label=f"{name}{half}"))
                return done

            def head(following):
                if following:
                    got = load_qkv([Prev("v project1")], lambda i: wqkv[i + 1, :, :, :, :])
                    got_wo = f.dma([Prev("out")], "sp", "wo", wo[:, :], lambda i: wo1[i, :, :])
                else:
                    got_wo = f.dma([Prev("out")], "sp", "wo", wo[:, :], wo1[H1 - 1, :, :])
                qk = [Prev(f"{name}{half}") for name in "qk" for half in range(2)]
                ts = []
                for half in range(2):
                    ts.append(f.pe(qk + [Prev(f"sums{half}")], [
                        mm(sbank[half][:, b * P:(b + 1) * P], qT[:, (4 * half + b) * P:(4 * half + b + 1) * P],
                           kT[:, (4 * half + b) * P:(4 * half + b + 1) * P]) for b in range(4)]))
                halves = [slice(0, 4), slice(4, 8)]
                te = []
                for half, hs in enumerate(halves):
                    s3 = sbank[half].rearrange("p (b t) -> p b t", b=4)
                    t = f.dve([ts[half]], dve.tensor_reduce, top[:, hs], s3, AX.X, ALU.max)
                    t = f.dve([t, Prev("column sums1")], dve.tensor_tensor, soft[:, hs, :], s3, spread(top[:, hs], P, 2), ALU.subtract)
                    te.append(f.act([t], act.activation, soft[:, hs, :], soft[:, hs, :], ACT.Exp, scale=HD1 ** -0.5))
                if following:
                    tq = project(0, got, [ts[1]], [[Prev("v0")], [Prev("v1")]])
                    tk = project(1, got, [ts[1]], [[tq[0]], [tq[1]]])
                tsum = []
                for half, hs in enumerate(halves):
                    t = f.dve([te[half]], dve.tensor_reduce, rsum[:, hs], soft[:, hs, :], AX.X, ALU.add)
                    t = f.dve([t], dve.reciprocal, rsum[:, hs], rsum[:, hs])
                    t = f.dve([t], dve.tensor_copy, rows[:, hs, :], spread(rsum[:, hs], P, 2))
                    t = f.pe([t], [mm(sbank[half][:, b * P:(b + 1) * P], rows[:, 4 * half + b, :], soft[:, 4 * half + b, :])
                                   for b in range(4)], label=f"column sums{half}")
                    t = f.act([t], act.copy, sums[:, 512 * half:512 * half + 512], sbank[half], label=f"sums{half}")
                    tsum.append(f.dve([t, Prev(f"v{half}"), Prev("out")], dve.tensor_tensor, oT[:, 512 * half:512 * half + 512],
                                      vT[:, 512 * half:512 * half + 512], sums[:, 512 * half:512 * half + 512], ALU.mult))
                if following:
                    project(2, got, [tsum[1]], [[tk[0]], [tk[1]]])
                f.pe([tsum[1], got_wo], [mm(y[b], oT[:, b * P:(b + 1) * P], wo[:, :], start=False, stop=not following and b % 2 == 1)
                                         for b in range(NSEQ)], label="out")

            t = f.dve([], dve.memset, soft[:, 0:4, :], 0.0)
            for k in range(4):
                f.pe([t], [mm(ps[:, k, :], soft[:, 0, :], soft[:, 0:4, :].rearrange("p a b -> p (a b)"), stop=False)])
            got = load_qkv([], wqkv[0, :, :, :, :])
            free = [[], []]
            for which in range(3):
                free = [[t] for t in project(which, got, [], free)]
            f.play()
            head(True)
            f.play(H1 - 1)
            head(False)
            f.play(join=False)

            t = None
            for k in range(4):
                x = x_all[:, 2 * k:2 * k + 2, :].rearrange("p b d -> p (b d)")
                t = f.dve([], dve.tensor_tensor, x, x, ps[:, k, :], ALU.add)
            for b in range(NSEQ):
                ts = f.dve([t], dve.bn_stats, stats[:, b, :], x_all[:, b, :])
            for b in range(NSEQ):
                t = f.dve([ts], dve.bn_aggr, mv[:, b, :], stats[:, b, :])
            t = f.dve([t], dve.tensor_scalar, var[:, :], mv[:, :, 1], EPS, None, ALU.add)
            tr_ = f.pool([t], pool.tensor_tensor, rstd[:, :], var[:, :], power[:, 0:NSEQ], ALU.pow)
            for b in range(NSEQ):
                f.dve([tr_], dve.tensor_scalar, x_all[:, b, :], x_all[:, b, :], mv[:, b, 0:1], rstd[:, b:b + 1],
                      ALU.subtract, ALU.mult)
            f.play()
            c.close()

        attention1()
        dump("x4", x_all[:, :, :])

        gate_sb = sb("gate_sb", [P, KD, NE])
        first_slot = sb("first_slot", [P, NE])
        chosen_before = sb("chosen_before", [P, NE], BF16)
        slot_all = sb("slot_all", [P, NSEQ, NE])
        weight_all = sb("weight_all", [P, NSEQ, TOPK])

        def cross1():
            c = ExitStack()

            def sb(name, shape, dt=F32):
                return c.enter_context(nc.sbuf_tensor(name, shape, dt))

            lanes = []
            for n in range(LANES):
                s = lambda name, shape, dt=F32, n=n: sb(f"{name}c_{n}", shape, dt)
                lanes.append(dict(
                    n=n, bank=[ps[:, 4 * n + k, :] for k in range(4)], flat=ps[:, 4 * n:4 * n + 4, :],
                    x=s("x", [P, D]), ctx=s("ctx", [P, D]), kheads=s("kheads", [P, HX, D]),
                    vheads=s("vheads", [P, 2, HX * (P + HDX)]), soft=s("soft", [P, HX, D]),
                    pT=s("pT", [P, HX, D]), top=s("top", [P, HX]), rsum=s("rsum", [P, HX]),
                    res=s("res", [P, D]), x5=s("x5", [P, D]), x5T=s("x5T", [P, KD, P]),
                    prob=s("prob", [P, NE]), left=s("left", [P, NE]), slot=s("slot", [P, NE]),
                    chosen=s("chosen", [P, NE], BF16), best=s("best", [P, TOPK]), slots=s("slots", [P, TOPK]),
                    index=s("index", [P, TOPK], U32), weight=s("weight", [P, TOPK]), one=s("one", [P, 4]),
                    token=s("token", [P, 1], I32), zero=s("zero", [P, 1], I32), spare=s("spare", [P, 1], U32), junk=s("junk", [P, TOPK, NE]),
                    stats=s("stats", [P, 6]), mv=s("mv", [P, 4]), chain={}))

            def scatter(after, part, lane, index, value, label=None):
                return f.step("pool", after, [(pool.indirect_dma_start, (
                    id_parts[part], bass.IndirectOffsetOnAxis(ap=index, axis=0), value, None), {})], label, f"part{part}lane{lane}", apart=True)

            f.dma([], "sp", "gate", gate_sb[:, :, :], gatew)
            f.pool([], pool.iota, first_slot[:, :], pattern=[[ROWS, NE]], base=1, channel_multiplier=0,
                   allow_small_or_imprecise_dtypes=True)
            f.dve([], dve.memset, chosen_before[:, :], 0.0)
            for L in lanes:
                f.dve([], dve.memset, L["vheads"][:, :, :], 0.0)
                t = f.pool([], pool.iota, L["token"][:, :], pattern=[[0, 1]], base=(L["n"] - LANES) * P, channel_multiplier=1)
                tz = f.dve([], dve.memset, L["zero"][:, :], 0)
                ti = f.pool([], pool.iota, L["spare"][:, :], pattern=[[0, 1]], base=TABLE - P, channel_multiplier=1)
                for k in range(PARTS):
                    first = scatter([tz, ti] + ([L["chain"][k]] if L["chain"] else []), k, L["n"], L["spare"][:, :], L["zero"][:, :])
                    for M in lanes[L["n"] + 1:]:
                        M["chain"][k] = first
            f.play()

            for name, src, readers, many in (("x", x_all, ["residual"], False), ("ctx", ctx_in, ["kheads", "ctxT"], True)):
                for L in lanes:
                    n = L["n"]
                    L["got " + name] = f.dma(
                        [Prev(f"{r}{n}") for r in readers], "sp", f"{name}c{n}",
                        L[name][:, :] if many else L[name][:, :].unsqueeze(1),
                        (lambda i, n=n: ctx_in[LANES * i + n, :, :]) if many else
                        (lambda i, n=n: x_all[:, bass.ds(LANES * i + n, 1), :]))

            def sequence(L):
                n, bank = L["n"], L["bank"]
                x, soft = L["x"], L["soft"]
                tkh = f.pool([L["got ctx"], Prev(f"scores{n}")], pool.tensor_tensor, L["kheads"][:, :, :],
                             spread(L["ctx"][:, :], HX, 1), spread(headmask[:, :], D, 2), ALU.mult, label=f"kheads{n}")
                t = f.pe([L["got ctx"], Prev(f"free0{n}")], [tr(bank[0][:, k * P:(k + 1) * P], L["ctx"][:, k * P:(k + 1) * P]) for k in range(2)],
                         label=f"ctxT{n}")
                tv = f.dve([t, Prev(f"weighted{n}")], dve.tensor_copy,
                           L["vheads"][:, :, :].rearrange("p k (h s) -> p k h s", s=P + HDX)[:, :, :, 0:HDX],
                           bank[0][:, 0:D].rearrange("p (k h s) -> p k h s", k=2, h=HX))
                yield
                free = [[tv], [Prev(f"free1{n}")], [Prev(f"free2{n}")], [Prev(f"free3{n}")]]
                for m in range(2):
                    ts = [f.pe([L["got x"], tkh] + free[k], [mm(bank[k], x[:, m * P:(m + 1) * P],
                                                                L["kheads"][:, 2 * k:2 * k + 2, :].rearrange("p a b -> p (a b)"))],
                               label=f"scores{n}") for k in range(4)]
                    yield
                    te = []
                    for k in range(4):
                        s3 = bank[k].rearrange("p (h t) -> p h t", h=2)
                        t = f.dve([ts[k]], dve.tensor_reduce, L["top"][:, 2 * k:2 * k + 2], s3, AX.X, ALU.max)
                        t = f.dve([t], dve.tensor_scalar, L["top"][:, 2 * k:2 * k + 2], L["top"][:, 2 * k:2 * k + 2],
                                  -HDX ** -0.5, None, ALU.mult)
                        for h in range(2):
                            te.append(f.act([t, Prev(f"probT{n}")] if m == 0 else [t], act.activation, soft[:, 2 * k + h, :], s3[:, h, :], ACT.Exp,
                                            bias=L["top"][:, 2 * k + h:2 * k + h + 1], scale=HDX ** -0.5,
                                            accum_out=L["rsum"][:, 2 * k + h:2 * k + h + 1]))
                        if k % 2:
                            yield
                    tn = []
                    for k in range(2):
                        hs = slice(4 * k, 4 * k + 4)
                        t = f.dve([te[4 * k + 3]], dve.reciprocal, L["rsum"][:, hs], L["rsum"][:, hs])
                        tn.append(f.dve([t], dve.tensor_tensor, soft[:, hs, :], soft[:, hs, :], spread(L["rsum"][:, hs], D, 2), ALU.mult))
                        yield
                    tp = []
                    for k in range(4):
                        t = f.pe([tn[k // 2]], [tr(bank[k][:, (2 * h + u) * P:(2 * h + u + 1) * P], soft[:, 2 * k + h, u * P:(u + 1) * P])
                                                for h in range(2) for u in range(2)], label=f"probT{n}")
                        dst = L["pT"][:, 2 * k:2 * k + 2, :].rearrange("p a b -> p (a b)")
                        tp.append(f.act([t], act.copy, dst, bank[k]) if k % 2 else f.dve([t], dve.tensor_copy, dst, bank[k]))
                        if k % 2:
                            yield
                    t = f.pe([tp[2], tp[3], tv], [mm(bank[0][:, 0:P], L["vheads"][:, u, h * P:(h + 1) * P], L["pT"][:, h, u * P:(u + 1) * P],
                                                     start=h == 0 and u == 0, stop=h == HX - 1 and u == 1)
                                                  for h in range(HX) for u in range(2)], label=f"weighted{n}")
                    t = f.dve([t], dve.tensor_tensor, L["res"][:, m * P:(m + 1) * P], bank[0][:, 0:P], x[:, m * P:(m + 1) * P],
                              ALU.add, label=f"residual{n}")
                    free = [[t], [tp[1]], [tp[2]], [tp[3]]]
                    yield
                t5 = norm(L, L["res"][:, :], L["x5"][:, :], [t, Prev(f"x5 out{n}")])
                f.dma([t5], "act", f"x5{n}", lambda i: x5_rows[bass.ds((LANES * i + n) * P, P), :], L["x5"][:, :], label=f"x5 out{n}")
                yield
                t = f.pe([t5, tp[1]], [tr(bank[1][:, k * P:(k + 1) * P], L["x5"][:, k * P:(k + 1) * P]) for k in range(KD)])
                t = f.act([t], act.copy, L["x5T"][:, :, :].rearrange("p k t -> p (k t)"), bank[1][:, 0:D], label=f"free1{n}")
                t = f.pe([t, tp[2]], [mm(bank[2][:, 0:NE], L["x5T"][:, k, :], gate_sb[:, k, :], start=k == 0, stop=k == KD - 1)
                                      for k in range(KD)])
                one = L["one"]
                t = f.dve([t], dve.tensor_reduce, one[:, 0:1], bank[2][:, 0:NE], AX.X, ALU.max, negate=True)
                t = f.act([t], act.activation, L["prob"][:, :], bank[2][:, 0:NE], ACT.Exp, bias=one[:, 0:1], accum_out=one[:, 1:2],
                          label=f"free2{n}")
                t = f.dve([t], dve.reciprocal, one[:, 2:3], one[:, 1:2])
                yield
                t = f.dve([t], dve.tensor_scalar, L["prob"][:, :], L["prob"][:, :], one[:, 2:3], None, ALU.mult)
                t = f.dve([t], dve.max, L["best"][:, :], L["prob"][:, :], apart=True)
                t = f.dve([t], dve.match_replace, L["left"][:, :], L["best"][:, :], L["prob"][:, :], -1.0, apart=True)
                tc = f.dve([t], dve.tensor_scalar, L["chosen"][:, :], L["left"][:, :], 0.0, None, ALU.is_lt)
                t = f.pe([tc, tp[3]] + ([L["counted"]] if L["counted"] else [Prev("counted")]), [
                    mm(bank[3][:, 0:NE], before[:, :], L["chosen"][:, :], stop=False),
                    mm(bank[3][:, 0:NE], onesb[:, :], chosen_before[:, :], start=False)])
                counted = f.dve([t], dve.tensor_tensor, chosen_before[:, :], chosen_before[:, :], L["chosen"][:, :], ALU.add,
                                label="counted")
                for M in lanes[n + 1:n + 2]:
                    M["counted"] = counted
                t = f.dve([t, Prev(f"slot out{n}")], dve.tensor_tensor, L["slot"][:, :], bank[3][:, 0:NE], first_slot[:, :], ALU.add, label=f"free3{n}")
                t = f.dve([t], dve.tensor_tensor, L["slot"][:, :], L["slot"][:, :], L["chosen"][:, :], ALU.mult)
                f.dma([t], "act", f"slot{n}", lambda i: slot_all[:, bass.ds(LANES * i + n, 1), :], L["slot"][:, :].unsqueeze(1), label=f"slot out{n}")
                yield
                t = f.dve([t], dve.max, L["slots"][:, :], L["slot"][:, :], apart=True)
                ti = f.dve([t] + [Prev(f"scattered{k}lane{n}") for k in range(PARTS)], dve.tensor_scalar, L["index"][:, :], L["slots"][:, :], -1.0, None, ALU.add)
                tt = f.dve([], dve.tensor_scalar, L["token"][:, :], L["token"][:, :], float(LANES * P), None, ALU.add)
                for j in range(TOPK):
                    k = j % PARTS
                    before_it = chain[k] if k in chain else Prev(f"scattered{k}lane{LANES - 1}")
                    chain[k] = scatter([ti, tt, before_it], k, n, L["index"][:, j:j + 1], L["token"][:, :], f"scattered{k}lane{n}")
                for j in range(TOPK):
                    tw = f.dve([t, Prev(f"weight out{n}")], dve.scalar_tensor_tensor, out=L["junk"][:, j, :], in0=L["slot"][:, :], scalar=L["slots"][:, j:j + 1],
                               in1=L["prob"][:, :], op0=ALU.is_equal, op1=ALU.mult, accum_out=L["weight"][:, j:j + 1])
                f.dma([tw], "act", f"weight{n}", lambda i: weight_all[:, bass.ds(LANES * i + n, 1), :], L["weight"][:, :].unsqueeze(1), label=f"weight out{n}")
                f.dve([t], dve.tensor_copy, one[:, 3:4], one[:, 2:3], label=f"free0{n}")
                yield

            chain = {}
            for L in lanes:
                L["counted"] = None
            interleave(*[sequence(L) for L in lanes])
            f.play(NSEQ // LANES)
            c.close()

        cross1()
        dump("x5", x5_rows)
        dump("weights", weight_all[:, :, :])
        for k in range(PARTS if debug and "ids" in debug else 0):
            f.dma([], "sp", "dbg", debug["ids"][k:k + 1, :].rearrange("a n -> (a n)"), id_parts[k].rearrange("n o -> (n o)"))
            f.play()

        index_all = sb("index_all", [P, NSEQ, TOPK], U32)
        tile_expert = sb("tile_expert", [1, NT + 2 * TPT], I32)
        tile_ids = sb("tile_ids", [P, NT + 2 * TPT], U32)

        def plan():
            c = ExitStack()

            def sb(name, shape, dt=F32):
                return c.enter_context(nc.sbuf_tensor(name, shape, dt))

            upto = sb("upto", [NE, NE], BF16)
            tiles = sb("tiles", [NE, P])
            count = sb("count", [NE, P])
            tilesb = sb("tilesb", [NE, P], BF16)
            base, end, mine = sb("base", [P, NE]), sb("end", [P, NE]), sb("mine", [P, NE])
            shift, expert_no = sb("shift", [P, NE]), sb("expert_no", [P, NE])
            tile_no = sb("tile_no", [P, 1])
            hit, cols = sb("hit", [P, 2, NE]), sb("cols", [P, 6])
            plan_i, line = sb("plan_i", [P, 1], I32), sb("line", [P, 1], U32)
            by_tile, by_tilef = sb("by_tile", [NT, P], I32), sb("by_tilef", [NT, P])
            moved, is_in = sb("moved", [P, NSEQ, NE]), sb("is_in", [P, NSEQ, NE])
            best = sb("bestp", [P, NSEQ, TOPK])
            part = sb("part", [P, PARTS, TABLE // P], I32)

            tl = [f.dma([], "sp", "merge", part[:, k, :], id_parts[k].rearrange("(p n) o -> p (n o)", p=P)) for k in range(PARTS)][-1]
            t = f.dve([tl], dve.tensor_tensor, part[:, 0:2, :], part[:, 0:2, :], part[:, 2:4, :], ALU.add)
            t = f.dve([t], dve.tensor_tensor, part[:, 0, :], part[:, 0, :], part[:, 1, :], ALU.add)
            t_table = f.dma([t], "sp", "merge", ids_table.rearrange("(p n) o -> p (n o)", p=P), part[:, 0, :])

            g = f.pool([], pool.affine_select, out=upto[:, :], in_=onesb[0:NE, 0:NE], compare_op=ALU.is_ge, fill=0.0,
                       base=0, pattern=[[1, NE]], channel_multiplier=-1)
            g = f.pool([], pool.iota, tile_no[:, :], pattern=[[0, 1]], base=0, channel_multiplier=1,
                       allow_small_or_imprecise_dtypes=True)
            g = f.pool([], pool.iota, expert_no[:, :], pattern=[[1, NE]], base=0, channel_multiplier=0,
                       allow_small_or_imprecise_dtypes=True)
            t = f.pe([], [mm(ps[0:NE, 0, 0:P], chosen_before[:, :], onesb[:, :])])
            tc = f.dve([t], dve.tensor_copy, count[:, :], ps[0:NE, 0, 0:P])
            t = f.dve([tc], dve.tensor_scalar, tiles[:, :], count[:, :], 0.0, None, ALU.is_gt)
            for k in range(1, ROWS // P):
                t = f.dve([t], dve.scalar_tensor_tensor, out=tiles[:, :], in0=count[:, :], scalar=float(k * P), in1=tiles[:, :],
                          op0=ALU.is_gt, op1=ALU.add)
            t = f.dve([t], dve.tensor_copy, tilesb[:, :], tiles[:, :])
            t = f.pe([t, g], [mm(ps[:, 1, 0:NE], tilesb[:, :], before[0:NE, 0:NE]), mm(ps[:, 1, NE:2 * NE], tilesb[:, :], upto[:, :])])
            t = f.dve([t], dve.tensor_copy, base[:, :], ps[:, 1, 0:NE])
            te = f.dve([], dve.tensor_copy, end[:, :], ps[:, 1, NE:2 * NE])
            t = f.dve([te], dve.tensor_tensor, mine[:, :], end[:, :], base[:, :], ALU.subtract)
            t = f.dve([t], dve.tensor_scalar, hit[:, 0, :], end[:, :], tile_no[:, 0:1], 0.0, ALU.is_le, ALU.add, accum_out=cols[:, 0:1])
            t2 = f.dve([], dve.scalar_tensor_tensor, out=hit[:, 1, :], in0=end[:, :], scalar=tile_no[:, 0:1], in1=mine[:, :],
                       op0=ALU.is_le, op1=ALU.mult, accum_out=cols[:, 1:2])
            t = f.dve([t2], dve.tensor_tensor, cols[:, 2:3], tile_no[:, :], cols[:, 1:2], ALU.subtract)
            ti = f.dve([t], dve.scalar_tensor_tensor, out=line[:, :], in0=cols[:, 0:1], scalar=float(ROWS // P), in1=cols[:, 2:3],
                       op0=ALU.mult, op1=ALU.add)
            t = f.dve([ti], dve.tensor_scalar, plan_i[:, :], cols[:, 0:1], float(NE - 1), None, ALU.min)
            t = f.dma([t], "sp", "plan", tile_expert_dram, plan_i[:, :])
            f.dve([], dve.memset, tile_expert[:, NT:], 0)
            f.dve([], dve.memset, tile_ids[:, NT:], 0)
            f.dma([t], "sp", "plan", tile_expert[:, 0:NT], tile_expert_dram.rearrange("t c -> (t c)").unsqueeze(0))
            t = f.step("pool", [ti, t_table], [(pool.indirect_dma_start, (
                by_tile[:, :], None, ids_table.rearrange("(l s) o -> l (s o)", s=P), bass.IndirectOffsetOnAxis(ap=line[:, :], axis=0)), {})],
                None, "lines")
            t = f.dve([t], dve.tensor_copy, by_tilef[:, :], by_tile[:, :])
            t = f.pe([t], [tr(ps[:, 2, 0:NT], by_tilef[:, :])])
            f.dve([t], dve.tensor_copy, tile_ids[:, 0:NT], ps[:, 2, 0:NT])
            t = f.dve([], dve.tensor_scalar, shift[:, :], base[:, :], float(P), float(LAG * P), ALU.mult, ALU.add)
            t = f.dve([t, g], dve.scalar_tensor_tensor, out=shift[:, :], in0=expert_no[:, :], scalar=-float(ROWS), in1=shift[:, :],
                      op0=ALU.mult, op1=ALU.add)
            t1 = f.dve([t], dve.tensor_tensor, moved[:, :, :], slot_all[:, :, :], spread(shift[:, :], NSEQ, 1), ALU.add)
            t = f.dve([t1], dve.scalar_tensor_tensor, out=is_in[:, :, :], in0=slot_all[:, :, :], scalar=0.0, in1=moved[:, :, :],
                      op0=ALU.is_gt, op1=ALU.mult)
            for b in range(NSEQ):
                tb = f.dve([t], dve.max, best[:, b, :], is_in[:, b, :])
            f.dve([tb], dve.tensor_scalar, index_all[:, :, :], best[:, :, :], -1.0, None, ALU.add)
            f.play()
            f.join()
            c.close()

        plan()

        def experts():
            c = ExitStack()

            def sb(name, shape, dt=F32):
                return c.enter_context(nc.sbuf_tensor(name, shape, dt))

            tiles = []
            for u in range(TPT):
                s = lambda name, shape, dt=F32, u=u: sb(f"{name}_e{u}", shape, dt)
                tiles.append(dict(w=s("w", [P, WCOLS]), rows=s("rows", [P, D]), xT=s("xT", [P, KD, P]),
                                  gate=s("gate", [P, P]), h=s("h", [P, P]), o=s("o", [P, D]),
                                  t_bank=ps[:, u % 2, :], g_bank=ps[:, 2 + u % 2, :], o_bank=ps[:, 4 + u % 2, :]))
            half = TPT // 2
            ids = [sb(f"ids{k}", [P, half], U32) for k in range(2)]
            latest = f.latest
            experts_of_turn = []

            def read_experts(i):
                experts_of_turn[:] = read(tile_expert[0:1, bass.ds(TPT * i + TPT - LAG, TPT)])
                return tile_ids[:, bass.ds(TPT * i + TPT - LAG + half, half)]

            def read(ap):
                return nc.values_load_multi_w_load_instructions(
                    ap, engines=[mybir.EngineType.SP], min_val=0, max_val=NE - 1,
                    skip_runtime_bounds_check_because="the plan keeps them below the number of experts")[1]

            def ids_in(k, source):
                return f.dma([latest(f"got rows{(half * k + s - LAG) % TPT}") for s in range(half)], "sp", f"ids{k}", ids[k][:, :],
                             source, label=f"ids{k}")

            def fetch(s):
                u, (k, col) = (s - LAG) % TPT, divmod(s, half)
                f.dma([latest(f"down{u}")], "sp", f"w{u}", tiles[u]["w"][:, :],
                      lambda i: we[bass.ds(experts_of_turn[s], 1), :, :].rearrange("a p n -> (a p) n"), label=f"got w{u}")
                f.step("pool", [latest(f"ids{k}"), latest(f"turned{u}")], [(pool.indirect_dma_start, (
                    tiles[u]["rows"][:, :], None, x5_rows, bass.IndirectOffsetOnAxis(ap=ids[k][:, col:col + 1], axis=0)), {})],
                    f"got rows{u}", f"rows{u}", apart=True)

            def turn(u):
                T = tiles[u]
                t = f.pe([latest(f"got rows{u}"), latest(f"rowsT{(u - 2) % TPT}")], [
                    tr(T["t_bank"][:, k * P:(k + 1) * P], T["rows"][:, k * P:(k + 1) * P]) for k in range(KD)], label=f"turned{u}")
                f.act([t, latest(f"up{u}")], act.copy, T["xT"][:, :, :].rearrange("p k t -> p (k t)"), T["t_bank"][:, 0:D], label=f"rowsT{u}")

            def up(u):
                T = tiles[u]
                w13 = T["w"][:, 0:KD * 2 * INTER].rearrange("p (k n) -> p k n", k=KD)
                t = f.pe([latest(f"rowsT{u}"), latest(f"got w{u}"), latest(f"h{(u - 2) % TPT}")], [
                    mm(T["g_bank"][:, j * P:(j + 1) * P], w13[:, k, j * INTER:(j + 1) * INTER], T["xT"][:, k, :], start=k == 0, stop=k == KD - 1)
                    for j in range(2) for k in range(KD)], label=f"up{u}")
                t = f.act([t, latest(f"h{u}")], act.activation, T["gate"][:, :], T["g_bank"][:, 0:P], ACT.Silu)
                f.dve([t, latest(f"down{u}")], dve.tensor_tensor, T["h"][:, :], T["g_bank"][:, P:2 * P], T["gate"][:, :], ALU.mult, label=f"h{u}")

            def down(u, block):
                T = tiles[u]
                t = f.pe([latest(f"h{u}"), latest(f"o{(u - 2) % TPT}")], [
                    mm(T["o_bank"][:, 0:D], T["h"][:, :], T["w"][:, KD * 2 * INTER:])], label=f"down{u}")
                t = f.dve([t, latest(f"stored{u}")], dve.tensor_copy, T["o"][:, :], T["o_bank"][:, 0:D], label=f"o{u}")
                f.dma([t], "sp", f"stored{u}", lambda i: expert_rows[bass.ds(block(i) * P, P), :], T["o"][:, :], label=f"stored{u}")

            for T in tiles[TPT - LAG:]:
                f.dve([], dve.memset, T["w"][:, :], 0.0)
                f.dve([], dve.memset, T["h"][:, :], 0.0)
                t = f.dve([], dve.memset, T["xT"][:, :, :], 0.0)
            first = read(tile_expert[0:1, 0:TPT - LAG])
            for u in range(TPT - LAG):
                f.dma([], "sp", f"w{u}", tiles[u]["w"][:, :], we[bass.ds(first[u], 1), :, :].rearrange("a p n -> (a p) n"))
                f.step("pool", [], [(pool.indirect_dma_start, (
                    tiles[u]["rows"][:, :], None, x5_rows, bass.IndirectOffsetOnAxis(ap=tile_ids[:, u:u + 1], axis=0)), {})],
                    None, f"rows{u}")
            f.dma([], "sp", "ids0", ids[0][:, :], tile_ids[:, TPT - LAG:TPT - LAG + half])
            for u in range(TPT - LAG, TPT):
                f.step("pool", [], [(pool.indirect_dma_start, (
                    tiles[u]["rows"][:, :], None, x5_rows, bass.IndirectOffsetOnAxis(ap=tile_ids[:, u:u + 1], axis=0)), {})],
                    None, f"rows{u}")
            act.preload_act_table(ACT.Silu)
            f.play(join=False)

            ids_in(1, read_experts)
            for s in range(TPT):
                turn(s)
                up((s - 1) % TPT)
                down((s - LAG) % TPT, lambda i, s=s: TPT * i + s)
                fetch(s)
                if s == half - 1:
                    ids_in(0, lambda i: tile_ids[:, bass.ds(TPT * i + 2 * TPT - LAG, half)])
            f.play(NT // TPT)
            up(TPT - 1)
            down(TPT - 2, lambda i: NT)
            down(TPT - 1, lambda i: NT + 1)
            f.play()
            c.close()

        experts()

        def combine():
            c = ExitStack()

            def sb(name, shape, dt=F32):
                return c.enter_context(nc.sbuf_tensor(name, shape, dt))

            lanes = []
            for n in range(LANES):
                s = lambda name, shape, dt=F32, n=n: sb(f"{name}o_{n}", shape, dt)
                lanes.append(dict(n=n, x5=s("x5", [P, D]), index=s("index", [P, TOPK], U32), weight=s("weight", [P, TOPK]),
                                  rows=s("rows", [P, TOPK, D]), acc=s("acc", [P, D]), y=s("y", [P, D]),
                                  stats=s("stats", [P, 6]), mv=s("mv", [P, 4])))

            def sequence(L):
                n = L["n"]
                seq = lambda src: (lambda i: src[:, bass.ds(LANES * i + n, 1), :])
                summed = Prev(f"summed{n}")
                ti = f.dma([summed], "sp", f"oi{n}", L["index"][:, :].unsqueeze(1), seq(index_all))
                f.dma([summed], "sp", f"ox{n}", L["x5"][:, :], lambda i: x5_rows[bass.ds((LANES * i + n) * P, P), :])
                tx = f.dma([summed], "sp", f"ox{n}", L["weight"][:, :].unsqueeze(1), seq(weight_all))
                got = []
                for j in range(TOPK):
                    got.append(f.step("pool", [ti, summed], [(pool.indirect_dma_start, (
                        L["rows"][:, j, :], None, expert_rows, bass.IndirectOffsetOnAxis(ap=L["index"][:, j:j + 1], axis=0)), {})],
                        None, f"or{n}", apart=True))
                yield
                t = tx
                for j in range(TOPK):
                    src = L["x5"] if j == 0 else L["acc"]
                    t = f.dve([t, got[-1]], dve.scalar_tensor_tensor, out=L["acc"][:, :], in0=L["rows"][:, j, :], scalar=L["weight"][:, j:j + 1],
                              in1=src[:, :], op0=ALU.mult, op1=ALU.add, label=f"summed{n}")
                t = norm(L, L["acc"][:, :], L["y"][:, :], [t, Prev(f"y out{n}")])
                f.dma([t], "act", f"y{n}", lambda i: out[bass.ds(LANES * i + n, 1), :, :].rearrange("a p d -> (a p) d"), L["y"][:, :], label=f"y out{n}")
                yield

            interleave(*[sequence(L) for L in lanes])
            f.play(NSEQ // LANES)
            f.join()
            c.close()

        combine()


def layout(x, ctx_2048, L0_attn_Wq, L0_attn_Wk, L0_attn_Wv, L0_attn_Wo, L0_xattn_theta_w, L0_xattn_theta_b,
           L0_xattn_phi_w, L0_xattn_phi_b, L0_xattn_g_w, L0_xattn_g_b, L0_xattn_ln_gamma, L0_xattn_ln_beta,
           L0_xattn_out_w, L0_xattn_out_b, L0_ffn_w_up_q, L0_ffn_w_up_scale, L0_ffn_b_up, L0_ffn_w_up_lora_a,
           L0_ffn_w_up_lora_b, L0_ffn_w_down_q, L0_ffn_w_down_scale, L0_ffn_b_down, L0_ffn_w_down_lora_a,
           L0_ffn_w_down_lora_b, L1_attn_w_qkv, L1_attn_w_o, L1_ffn_gate_w, L1_ffn_w13, L1_ffn_w2):
    def rows(w):
        return w.reshape(-1, P, w.shape[-1]).transpose(1, 0, 2)

    qkv = L1_attn_w_qkv.reshape(KD, P, 3, H1, HD1).transpose(3, 1, 0, 2, 4)
    w13 = L1_ffn_w13.transpose(0, 2, 1).reshape(NE, KD, P, 2 * INTER).transpose(0, 2, 1, 3).reshape(NE, P, -1)
    w2 = L1_ffn_w2.transpose(0, 2, 1)
    arrays = dict(
        x_in=x, ctx_in=ctx_2048,
        w0=np.stack([rows(w.T) for w in (L0_attn_Wq, L0_attn_Wk, L0_attn_Wv, L0_attn_Wo)], 1),
        thw=np.stack([w.T for w in (L0_xattn_theta_w, L0_xattn_phi_w, L0_xattn_g_w)], 1),
        outw=L0_xattn_out_w.T,
        bias64=np.stack([L0_xattn_theta_b, L0_xattn_phi_b], 1),
        bias128=np.concatenate([L0_xattn_out_b[:, None], L0_ffn_b_up.reshape(FT, P).T], 1),
        gb=L0_xattn_g_b[None], gamma=L0_xattn_ln_gamma, beta=L0_xattn_ln_beta,
        upq=rows(L0_ffn_w_up_q.T), ups=L0_ffn_w_up_scale.T,
        upa=L0_ffn_w_up_lora_a.T, upb=L0_ffn_w_up_lora_b,
        dnq=rows(L0_ffn_w_down_q.T), dns=L0_ffn_w_down_scale.T, bdn=L0_ffn_b_down[None],
        dna=L0_ffn_w_down_lora_a.T, dnb=L0_ffn_w_down_lora_b,
        wqkv=qkv, wo1=L1_attn_w_o.reshape(H1, P, D), gatew=rows(L1_ffn_gate_w.T),
        we=np.concatenate([w13, w2], 2))
    return {n: np.ascontiguousarray(a) for n, a in arrays.items()}


def kernel(**inputs):
    import concourse.bacc as bacc
    from concourse.bass_utils import run_bass_kernel_spmd

    nc = bacc.Bacc("TRN2", target_bir_lowering=False, num_devices=1)
    arrays = {f"in_{name}": a for name, a in layout(**{k: np.asarray(v) for k, v in inputs.items()}).items()}
    args = [nc.dram_tensor(name, a.shape, mybir.dt.from_np(a.dtype), kind="ExternalInput").ap() for name, a in arrays.items()]
    out = nc.dram_tensor("out", (NSEQ, P, D), F32, kind="ExternalOutput").ap()
    decoder(nc, *args, out)
    result = run_bass_kernel_spmd(nc, [arrays], core_ids=[0])
    return result.results[0]["out"]
```

```python
from contextlib import ExitStack

import numpy as np

import concourse.bass as bass
from concourse import mybir

F32 = mybir.dt.float32
F32R = mybir.dt.float32r
BF16 = mybir.dt.bfloat16
I32 = mybir.dt.int32
U32 = mybir.dt.uint32
ALU = mybir.AluOpType
ACT = mybir.ActivationFunctionType
AX = mybir.AxisListType

P = 128
NSEQ = 8
D = 256
KD = D // P
TOK = NSEQ * P
LANES = 2
EPS = 1e-5

H0, HD0 = 16, 16
HP = P // HD0
LAT = 64
FF, FT = 1024, 8
QBLK, RANK = 64, 16
H1, HD1 = 16, 128
HX, HDX = 8, 16
NE, TOPK, INTER = 64, 8, 128
ROWS = TOK
NT = 128
TABLE = NE * ROWS + NT * P
ENDS = 2
TPT = 8
LAG = 2
PARTS = 4
WCOLS = KD * 2 * INTER + D


class Token:

    def __init__(self, play, name, amount, stage):
        self.play, self.name, self.amount, self.stage, self.at, self.final = play, name, amount, stage, None, None


class Prev:

    def __init__(self, label, turns=1):
        self.label, self.turns = label, turns


class Step:
    def __init__(self, engine, after, calls, token, apart):
        self.engine, self.after, self.calls, self.token, self.apart = engine, after, calls, token, apart


class Flow:

    def __init__(self, nc, ctx):
        self.nc, self.ctx = nc, ctx
        self.engines = {"pe": nc.tensor, "act": nc.scalar, "dve": nc.vector, "pool": nc.gpsimd, "sp": nc.sync}
        self.sems, self.total = {}, {}
        self.passed = ctx.enter_context(nc.semaphore("passed"))
        self.plays = 0
        self.begin()

    def begin(self):
        self.plays += 1
        self.steps, self.labels = [], {}

    def latest(self, label):
        return self.labels.get(label) or Prev(label)

    def step(self, engine, after, calls, label=None, stream=None, apart=False):
        name, amount = (stream, 16) if stream else (engine, 1)
        if name not in self.sems:
            self.sems[name] = self.ctx.enter_context(self.nc.semaphore("done_" + name))
            self.total[name] = 0
        token = Token(self.plays, name, amount, 0)
        if label:
            self.labels[label] = token
        self.steps.append(Step(engine, list(after), calls, token, apart or engine == "sp"))
        return token

    def pe(self, after, calls, label=None, apart=False):
        return self.step("pe", after, calls, label, apart=apart)

    def act(self, after, call, *args, label=None, **kw):
        return self.step("act", after, [(call, args, kw)], label)

    def dve(self, after, call, *args, label=None, apart=False, **kw):
        return self.step("dve", after, [(call, args, kw)], label, apart=apart)

    def pool(self, after, call, *args, label=None, **kw):
        return self.step("pool", after, [(call, args, kw)], label)

    def dma(self, after, engine, stream, out, in_, label=None):
        return self.step(engine, after, [(self.engines[engine].dma_start, (out, in_), {})], label, stream)

    def lanes(self, *lanes, order=None, split=None, last_after=None):
        pieces = []
        for lane in lanes:
            mine, kept = [], self.steps
            while True:
                self.steps = []
                more = next(lane, "end")
                mine.append(self.steps)
                if more == "end":
                    break
            self.steps = kept
            pieces.append(mine)
        for mine in pieces:
            if last_after is not None:
                for step in mine[-1]:
                    step.token.stage = 1
                mine[last_after + 1:] = [mine[-1]] + mine[last_after + 1:-1]
        if split:
            late = pieces[-1]
            for piece in late[split:]:
                for step in piece:
                    step.token.stage = 1
            pieces[-1] = late[split:] + late[:split]
        if order is None:
            order = "".join(str(n) for k in range(max(map(len, pieces))) for n, mine in enumerate(pieces) if k < len(mine))
        self.pieces = pieces
        rest = [iter(mine) for mine in pieces]
        for n in order:
            self.steps += next(rest[int(n)])
        assert all(next(mine, None) is None for mine in rest)

    def play(self, times=1, join=True, ahead=()):
        nc, steps = self.nc, self.steps
        if join:
            self.join(None if join is True else join, ahead)
        skewed = any(s.token.stage for s in steps)
        count = {}
        for s in steps:
            count[s.token.name] = count.get(s.token.name, 0) + s.token.amount
            s.token.at = count[s.token.name]
        for name, amount in count.items():
            if times > 1 and self.total[name] < amount + 1:
                owner = next(s.engine for s in steps if s.token.name == name)
                if owner == "pool" != name:
                    continue
                more = amount + 16 - amount % 16
                self.engines[owner].sem_inc(self.sems[name], more)
                self.total[name] += more
        base = dict(self.total)
        if skewed:
            for name in {s.token.name for s in steps if s.token.stage and s.engine == "pool" != s.token.name}:
                base[name] -= count[name]
        ending = {name: base[name] + times * amount for name, amount in count.items()}

        def value(token, stage, i, turn):
            back = 0
            if isinstance(token, Prev):
                back, label = token.turns, token.label
                token = self.before[label] if times == 1 else self.labels[label]
            if token.play != self.plays:
                return token.name, token.final, None
            back += stage - token.stage
            assert back >= 0
            if turn is None:
                c = base[token.name] + token.at - back * count[token.name]
                return token.name, i * count[token.name] + c, c
            if turn - back < 0:
                return token.name, None, None
            if turn == times and back == 0:
                return token.name, token.final, None
            c = base[token.name] + token.at + (turn - back) * count[token.name]
            return token.name, c, (c if times == 1 else None)

        def emit(i, turn=None, stages=(0, 1)):
            seen = {}
            for s in steps:
                eng, token, sem = self.engines[s.engine], s.token, self.sems[s.token.name]
                if token.stage not in stages:
                    if turn == 0 and not (s.engine == "pool" != token.name):
                        eng.wait_ge(sem, base[token.name] + token.at - token.amount)
                        eng.sem_inc(sem, token.amount)
                    continue
                if turn == times > 1:
                    ending[token.name] += token.amount
                    token.final = ending[token.name]
                for t in s.after:
                    name, v, c = value(t, token.stage, i, turn)
                    if v is None:
                        continue
                    if c is not None:
                        if (s.engine, name) in seen and seen[s.engine, name] >= c:
                            continue
                        seen[s.engine, name] = c
                    eng.wait_ge(self.sems[name], v)
                    if s.apart and turn is None:
                        eng.sem_inc(self.passed, 1)
                for call, args, kw in s.calls:
                    args = [a(i - token.stage if token.stage else i) if callable(a) else a for a in args]
                    last = call(*args, **kw)
                last.then_inc(sem, token.amount)

        for s in steps:
            s.token.final = base[s.token.name] + (times - 1) * count[s.token.name] + s.token.at
        if times == 1:
            emit(0, turn=0)
        elif not skewed:
            with nc.Fori(0, times) as i:
                emit(i)
        else:
            emit(0, turn=0, stages=(0,))
            with nc.Fori(1, times) as i:
                emit(i)
            emit(times, turn=times, stages=(1,))
        self.total.update(ending)
        self.before = self.labels
        self.begin()

    def join(self, names=None, ahead=()):
        for engine, eng in self.engines.items():
            for name, total in self.total.items():
                if engine not in ahead and total and (names is None or name in names):
                    eng.wait_ge(self.sems[name], total)

    def all_of(self, name):
        token = Token(0, name, 0, 0)
        token.final = self.total[name]
        return token


def spread(ap, n, axis):
    shape = list(ap.shape)
    return ap.unsqueeze(axis).broadcast_to(shape[:axis] + [n] + shape[axis:])


def decoder(nc, x_in, ctx_in, w0, thw, outw, bias64, bias128, gb, gamma, beta, upq, ups, upa, upb, dnq, dns, bdn, dna,
            dnb, wqkv, wo1, gatew, we, out):
    ctx = ExitStack()
    with ctx:
        def sb(name, shape, dt=F32):
            return ctx.enter_context(nc.sbuf_tensor(name, shape, dt))

        f = Flow(nc, ctx)
        pe, act, dve, pool = nc.tensor, nc.scalar, nc.vector, nc.gpsimd
        ps = ctx.enter_context(nc.psum_tensor("ps", [P, 8, 512], F32))

        def mm(out, lhsT, rhs, start=True, stop=True, shared=False):
            return (pe.matmul, (out, lhsT, rhs), dict(start=start, stop=stop, skip_group_check=shared))

        def tr(out, in_):
            return (pe.transpose, (out, in_, ident[:, :]), {})

        id_parts = [nc.dram_tensor(f"id_part{k}", (TABLE, 1), I32).ap() for k in range(PARTS)]
        x5_rows = nc.dram_tensor("x5_rows", (TOK, D), F32).ap()
        expert_rows = nc.dram_tensor("expert_rows", ((NT + LAG) * P, D), F32).ap()
        tile_expert_dram = nc.dram_tensor("tile_expert_dram", (NT, 1), I32).ap()

        ident = sb("ident", [P, P])
        identb = sb("identb", [P, P], BF16)
        onesb = sb("onesb", [P, P], BF16)
        before = sb("before", [P, P], BF16)
        future = sb("future", [P, 4, P], BF16)
        headmask = sb("headmask", [P, HP])
        power = sb("power", [P, 8])
        mean64 = sb("mean64", [LAT, LAT])

        x_all = sb("x_all", [P, NSEQ, D])
        xT_all = sb("xT_all", [P, KD, TOK])

        def constants():
            g = []
            g.append(f.pool([], pool.memset, ident[:, :], 0.0))
            g.append(f.pool([], pool.memset, onesb[:, :], 1.0))
            g.append(f.pool([], pool.memset, future[:, :, :], 0.0))
            g.append(f.pool([], pool.memset, headmask[:, :], HD0 ** -0.5))
            g.append(f.pool([], pool.memset, power[:, :], -0.5))
            g.append(f.pool([], pool.memset, mean64[:, :], 1.0 / LAT))
            t = f.pool(g, pool.affine_select, out=ident[:, :], in_=ident[:, :], compare_op=ALU.not_equal, fill=1.0,
                       base=0, pattern=[[-1, P]], channel_multiplier=1)
            f.pool([], pool.affine_select, out=before[:, :], in_=onesb[:, :], compare_op=ALU.is_gt, fill=0.0,
                   base=0, pattern=[[1, P]], channel_multiplier=-1)
            f.pool([], pool.affine_select, out=future[:, :, :], in_=future[:, :, :], compare_op=ALU.is_ge, fill=-1e30,
                   base=0, pattern=[[0, 4], [-1, P]], channel_multiplier=1)
            m = f.pool([], pool.affine_select, out=headmask[:, :], in_=headmask[:, :], compare_op=ALU.is_ge, fill=0.0,
                       base=0, pattern=[[-HD0, HP]], channel_multiplier=1)
            f.pool([m], pool.affine_select, out=headmask[:, :], in_=headmask[:, :], compare_op=ALU.is_ge, fill=0.0,
                   base=HD0 - 1, pattern=[[HD0, HP]], channel_multiplier=-1)
            f.dve([t], dve.tensor_copy, identb[:, :], ident[:, :])

        def norm(L, src, dst, after, label=None):
            t = f.dve(after, dve.bn_stats, L["stats"][:, :], src)
            t = f.dve([t], dve.bn_aggr, L["mv"][:, 0:2], L["stats"][:, :], apart=True)
            t = f.dve([t], dve.tensor_scalar, L["mv"][:, 2:3], L["mv"][:, 1:2], EPS, None, ALU.add)
            t = f.pool([t], pool.tensor_tensor, L["mv"][:, 3:4], L["mv"][:, 2:3], power[:, 0:1], ALU.pow)
            return f.dve([t], dve.tensor_scalar, dst, src, L["mv"][:, 0:1], L["mv"][:, 3:4], ALU.subtract, ALU.mult,
                         label=label)

        def layer0():
            c = ExitStack()

            def sb(name, shape, dt=F32):
                return c.enter_context(nc.sbuf_tensor(name, shape, dt))

            w0_sb = sb("w0_sb", [P, 4, KD, D])
            th_sb = sb("th_sb", [P, 3, LAT])
            outw_sb = sb("outw_sb", [LAT, P])
            b64_sb = sb("b64_sb", [LAT, 2])
            b128_sb = sb("b128_sb", [P, 1 + FT])
            gb_sb = sb("gb_sb", [P, LAT])
            gamma_sb = sb("gamma_sb", [LAT, D])
            beta_sb = sb("beta_sb", [LAT, D])
            bdn_sb = sb("bdn_sb", [P, D])
            wup = sb("wup", [P, KD, FF])
            wdn = sb("wdn", [P, FT, D])
            lanes = []
            for n in range(LANES):
                s = lambda name, shape, dt=F32, n=n: sb(f"{name}_{n}", shape, dt)
                lanes.append(dict(
                    n=n, bank=[ps[:, 4 * n + k, :] for k in range(4)],
                    x=s("x", [P, D]), ctx=s("ctx", [P, D]), xT=s("xT", [P, KD, P]), q=s("q", [P, KD, P]),
                    k=s("k", [P, KD, P]), kheads=s("kheads", [P, KD, HP, P]),
                    vheads=s("vheads", [P, KD, HP * (P + HD0)]), soft=s("soft", [P, H0, P]),
                    pT=s("pT", [P, H0, P]), top=s("top", [P, H0]), rsum=s("rsum", [P, H0]),
                    oT=s("oT", [P, KD, P]), res=s("res", [P, D]), x1=s("x1", [P, D]), x2=s("x2", [P, D]),
                    x3=s("x3", [P, D]), x3T=s("x3T", [P, KD, P]), cx=s("cx", [P, D]), theta=s("theta", [LAT, D]), phi=s("phi", [LAT, D]),
                    g=s("g", [P, 2, LAT]), e=s("e", [P, 2, D]), eT=s("eT", [P, 2, D]), h=s("h", [LAT, D]),
                    hs=s("hs", [LAT, 6]), hm=s("hm", [LAT, 8]), up=s("up", [P, FT, P]),
                    stats=s("stats", [P, 6]), mv=s("mv", [P, 4])))

            c2 = ExitStack()
            upq_sb = c2.enter_context(nc.sbuf_tensor("upq_sb", [P, KD, FF], I32))
            ups_sb = c2.enter_context(nc.sbuf_tensor("ups_sb", [P, KD, FF], F32))
            dnq_sb = c2.enter_context(nc.sbuf_tensor("dnq_sb", [P, FT, D], I32))
            dns_sb = c2.enter_context(nc.sbuf_tensor("dns_sb", [P, FT, D], F32))
            upa_sb = c2.enter_context(nc.sbuf_tensor("upa_sb", [RANK, D], F32))
            upb_sb = c2.enter_context(nc.sbuf_tensor("upb_sb", [RANK, FF], F32))
            dna_sb = c2.enter_context(nc.sbuf_tensor("dna_sb", [RANK, FF], F32))
            dnb_sb = c2.enter_context(nc.sbuf_tensor("dnb_sb", [RANK, D], F32))
            zero_ids = c2.enter_context(nc.sbuf_tensor("zero_ids", [P, TABLE // P], I32))

            def load(stream, dst, src, after=()):
                return f.dma(after, "sp", stream, dst, src)

            for dst, src in ((upa_sb, upa), (upb_sb, upb), (dna_sb, dna), (dnb_sb, dnb)):
                t_lora = load("lora", dst[:, :], src)
            t_q = {}
            for name, q_sb, q, s_sb, scale in (("q up", upq_sb, upq, ups_sb, ups), ("q down", dnq_sb, dnq, dns_sb, dns)):
                load(name, q_sb[:, :, :], q)
                for s in range(P // QBLK):
                    rows = scale.rearrange("(k s) n -> s k n", s=P // QBLK)[s:s + 1, :, :]
                    t_q[name] = load(name, s_sb[s * QBLK:(s + 1) * QBLK, :, :], rows.broadcast_to([QBLK] + list(rows.shape[1:])))
            load("w", w0_sb[:, :, :, :], w0)
            load("w", th_sb[:, :, :], thw)
            load("w", outw_sb[:, :], outw)
            load("w", b64_sb[:, :], bias64)
            load("w", b128_sb[:, :], bias128)
            load("w", gb_sb[:, :], gb.broadcast_to([P, LAT]))
            load("w", gamma_sb[:, :], gamma)
            load("w", beta_sb[:, :], beta)
            t_w = load("w", bdn_sb[:, :], bdn.broadcast_to([P, D]))
            constants()
            tz = f.dve([], dve.memset, zero_ids[:, :], 0)
            for part in id_parts:
                f.dma([tz, t_w], "act", "table", part.rearrange("(p n) o -> p (n o)", p=P), zero_ids[:, :])
            for L in lanes:
                f.dve([], dve.memset, L["vheads"][:, :, :], 0.0)
            t_ab = []
            for first, a, b, n in ((0, upa_sb, upb_sb, FF), (4, dna_sb, dnb_sb, D)):
                width = min(n, 512)
                for j in range(4):
                    calls = []
                    for o in range(0, 512, width):
                        k, c0 = divmod(j * 512 + o, n)
                        calls.append(mm(ps[:, first + j, o:o + width], a[:, k * P:(k + 1) * P], b[:, c0:c0 + width]))
                    t_ab.append(f.pe([t_lora], calls))
            for name, first, dst, q, s in (("q up", 0, wup, upq_sb, ups_sb), ("q down", 4, wdn, dnq_sb, dns_sb)):
                t = f.dve([t_q[name]], dve.scalar_tensor_tensor, out=dst[:, :, :], in0=q[:, :, :], scalar=7.5,
                          in1=s[:, :, :], op0=ALU.subtract, op1=ALU.mult)
                flat = dst[:, :, :].rearrange("p k n -> p (k n)")
                f.dve([t, t_ab[first + 3]], dve.tensor_tensor, flat, flat,
                      ps[:, first:first + 4, :].rearrange("p b n -> p (b n)"), ALU.add)
            f.play(join=False)
            c2.close()
            act.preload_act_table(ACT.Exp)

            def sequence(L):
                n, (b0, b1, b2, b3) = L["n"], L["bank"]

                def was(label):
                    return [Prev(f"{label}{n}")]

                x, soft = L["x"], L["soft"]
                t_x = f.dma(was("x read"), "sp", f"x{n}", x[:, :], lambda i: x_in[LANES * i + n, :, :])
                got_ctx = f.dma(was("ctx added") + was("ctx read"), "sp", f"ctx{n}", L["ctx"][:, :], lambda i: ctx_in[LANES * i + n, :, :])
                t = f.pe([t_x] + was("free0"), [tr(b0[:, k * P:(k + 1) * P], x[:, k * P:(k + 1) * P]) for k in range(KD)])
                txT = f.act([t], act.copy, L["xT"][:, :, :].rearrange("p k t -> p (k t)"), b0[:, 0:D])
                yield
                calls = []
                for which in range(2):
                    for m in range(KD):
                        for k in range(KD):
                            calls.append(mm(b1[:, (which * KD + m) * P:(which * KD + m + 1) * P],
                                            w0_sb[:, which, k, m * P:(m + 1) * P], L["xT"][:, k, :],
                                            start=k == 0, stop=k == KD - 1))
                tqk = f.pe([txT] + was("free1"), calls)
                tv = f.pe(was("free2"), [mm(b2[:, 0:D], L["xT"][:, k, :], w0_sb[:, 2, k, :], start=k == 0, stop=k == KD - 1)
                                         for k in range(KD)])
                yield
                tk = f.act([tqk], act.copy, L["k"][:, :, :].rearrange("p k t -> p (k t)"), b1[:, D:2 * D])
                tq = f.act([], act.copy, L["q"][:, :, :].rearrange("p k t -> p (k t)"), b1[:, 0:D])
                tkh = [f.pool([tk], pool.tensor_tensor, L["kheads"][:, m, :, :], spread(L["k"][:, m, :], HP, 1),
                              spread(headmask[:, :], P, 2), ALU.mult) for m in range(KD)]
                tvh = f.dve([tv], dve.tensor_copy,
                            L["vheads"][:, :, :].rearrange("p k (h s) -> p k h s", s=P + HD0)[:, :, :, 0:HD0],
                            b2[:, 0:D].rearrange("p (k h s) -> p k h s", k=KD, h=HP))
                yield
                free = {0: [txT], 1: [tq], 2: [tvh], 3: was("free3")}
                ts = []
                for m in range(KD):
                    for half in range(2):
                        k = 2 * m + half
                        ts.append(f.pe([tq, tkh[m]] + free[k], [
                            mm(L["bank"][k], identb[:, :], future[:, :, :].rearrange("p a b -> p (a b)"), stop=False),
                            mm(L["bank"][k], L["q"][:, m, :], L["kheads"][:, m, 4 * half:4 * half + 4, :].rearrange("p a b -> p (a b)"), start=False)]))
                    yield
                tsub = []
                for k in range(4):
                    hs = slice(4 * k, 4 * k + 4)
                    s3 = L["bank"][k].rearrange("p (h t) -> p h t", h=4)
                    t = f.dve([ts[k]], dve.tensor_reduce, L["top"][:, hs], s3, AX.X, ALU.max)
                    tsub.append(f.dve([t], dve.tensor_tensor, soft[:, hs, :], s3, spread(L["top"][:, hs], P, 2), ALU.subtract))
                    yield
                te = [f.act([tsub[2 * k + 1]], act.activation, soft[:, 8 * k:8 * k + 8, :], soft[:, 8 * k:8 * k + 8, :],
                            ACT.Exp) for k in range(2)]
                tn = []
                for k in range(2):
                    hs = slice(8 * k, 8 * k + 8)
                    t = f.dve([te[k]], dve.tensor_reduce, L["rsum"][:, hs], soft[:, hs, :], AX.X, ALU.add)
                    t = f.dve([t], dve.reciprocal, L["rsum"][:, hs], L["rsum"][:, hs])
                    tn.append(f.dve([t], dve.tensor_tensor, soft[:, hs, :], soft[:, hs, :], spread(L["rsum"][:, hs], P, 2), ALU.mult))
                    yield
                tp = []
                for k in range(4):
                    t = f.pe([tn[k // 2]], [tr(L["bank"][k][:, h * P:(h + 1) * P], soft[:, 4 * k + h, :]) for h in range(4)])
                    dst = L["pT"][:, 4 * k:4 * k + 4, :].rearrange("p a b -> p (a b)")
                    tp.append(f.act([t], act.copy, dst, L["bank"][k]) if k % 2 else f.dve([t], dve.tensor_copy, dst, L["bank"][k]))
                    yield
                t = f.pe([tp[1], tp[3], tp[2]], [
                    mm(b0[:, m * P:(m + 1) * P], L["vheads"][:, m, h * P:(h + 1) * P], L["pT"][:, m * HP + h, :],
                       start=h == 0, stop=h == HP - 1) for m in range(KD) for h in range(HP)])
                to = f.act([t], act.copy, L["oT"][:, :, :].rearrange("p k t -> p (k t)"), b0[:, 0:D])
                yield
                t = f.pe([to], [mm(b1[:, 0:D], L["oT"][:, k, :], w0_sb[:, 3, k, :], start=k == 0, stop=k == KD - 1)
                                for k in range(KD)])
                tr1 = f.dve([t], dve.tensor_tensor, L["res"][:, :], x[:, :], b1[:, 0:D], ALU.add, label=f"x read{n}")
                yield
                t1 = norm(L, L["res"][:, :], L["x1"][:, :], [tr1])
                tcx = f.pool([t1, got_ctx], pool.tensor_tensor, L["cx"][:, :], L["x1"][:, :], L["ctx"][:, :], ALU.add, label=f"ctx added{n}")
                yield
                t = f.pe([t1, to, got_ctx], [mm(b0[0:LAT, 0:D], th_sb[:, 0, :], L["ctx"][:, :]),
                                    mm(b0[0:LAT, D:2 * D], th_sb[:, 1, :], L["x1"][:, :])], label=f"ctx read{n}")
                tth = f.act([t], act.activation, L["theta"][:, :], b0[0:LAT, 0:D], ACT.Identity, bias=b64_sb[:, 0:1])
                tph = f.act([], act.activation, L["phi"][:, :], b0[0:LAT, D:2 * D], ACT.Identity, bias=b64_sb[:, 1:2])
                yield
                t = f.pe([tr1], [mm(b1[:, s * LAT:(s + 1) * LAT], L["x1"][:, s * P:(s + 1) * P], th_sb[:, 2, :]) for s in range(2)])
                tg = f.dve([t], dve.tensor_tensor, L["g"][:, :, :], b1[:, 0:2 * LAT].rearrange("p (s l) -> p s l", s=2),
                           spread(gb_sb[:, :], 2, 1), ALU.add)
                yield
                t = f.pe([tph, tp[2]], [mm(b2[:, s * D:(s + 1) * D], L["theta"][:, s * P:(s + 1) * P], L["phi"][:, :]) for s in range(2)])
                yield
                s3 = b2.rearrange("p (s t) -> p s t", s=2)
                tm = f.dve([t], dve.tensor_reduce, L["top"][:, 0:2], s3, AX.X, ALU.max, negate=True)
                yield
                te = [f.act([tm], act.activation, L["e"][:, s, :], s3[:, s, :], ACT.Exp, bias=L["top"][:, s:s + 1],
                            accum_out=L["rsum"][:, s:s + 1]) for s in range(2)]
                t = f.dve([te[1]], dve.reciprocal, L["rsum"][:, 0:2], L["rsum"][:, 0:2])
                tn = [f.dve([t], dve.tensor_scalar, L["e"][:, s, :], L["e"][:, s, :], L["rsum"][:, s:s + 1], None, ALU.mult)
                      for s in range(2)]
                yield
                t = f.pe([tn[1], tp[3]], [tr(b3[:, (2 * s + u) * P:(2 * s + u + 1) * P], L["e"][:, u, s * P:(s + 1) * P])
                                          for s in range(2) for u in range(2)])
                teT = f.act([t], act.copy, L["eT"][:, :, :].rearrange("p s t -> p (s t)"), b3)
                yield
                tt = f.pe([teT, tg, tph], [mm(b0[0:LAT, 0:D], L["g"][:, s, :], L["eT"][:, s, :], start=s == 0, stop=s == 1)
                                           for s in range(2)])
                hm = L["hm"]
                t = f.dve([tt], dve.bn_stats, L["hs"][:, :], b0[0:LAT, 0:D])
                t = f.dve([t], dve.bn_aggr, hm[:, 0:2], L["hs"][:, :], apart=True)
                t = f.dve([t], dve.scalar_tensor_tensor, out=hm[:, 1:2], in0=hm[:, 0:1], scalar=hm[:, 0:1], in1=hm[:, 1:2],
                          op0=ALU.mult, op1=ALU.add)
                yield
                t = f.pe([t, tg], [mm(b1[0:LAT, 0:2], mean64[:, :], hm[:, 0:2])], apart=True)
                t = f.dve([t], dve.tensor_copy, hm[:, 2:4], b1[0:LAT, 0:2])
                t = f.dve([t], dve.scalar_tensor_tensor, out=hm[:, 4:5], in0=hm[:, 2:3], scalar=hm[:, 2:3], in1=hm[:, 3:4],
                          op0=ALU.mult, op1=ALU.subtract)
                tmu = f.dve([t], dve.tensor_scalar, hm[:, 5:6], hm[:, 4:5], -1.0, EPS, ALU.mult, ALU.add)
                yield
                tvr = f.pool([tmu], pool.tensor_tensor, hm[:, 6:7], hm[:, 5:6], power[0:LAT, 0:1], ALU.pow)
                th = f.dve([tmu], dve.scalar_tensor_tensor, out=L["h"][:, :], in0=b0[0:LAT, 0:D], scalar=hm[:, 2:3],
                           in1=gamma_sb[:, :], op0=ALU.subtract, op1=ALU.mult)
                t = f.dve([th, tvr], dve.scalar_tensor_tensor, out=L["h"][:, :], in0=L["h"][:, :], scalar=hm[:, 6:7],
                          in1=beta_sb[:, :], op0=ALU.mult, op1=ALU.add)
                t = f.act([t], act.activation, L["h"][:, :], L["h"][:, :], ACT.Relu)
                yield
                t = f.pe([t, te[1]], [mm(b2[:, 0:D], outw_sb[:, :], L["h"][:, :])])
                tr2 = f.dve([t, tcx], dve.scalar_tensor_tensor, out=L["res"][:, :], in0=b2[:, 0:D], scalar=b128_sb[:, 0:1],
                            in1=L["cx"][:, :], op0=ALU.add, op1=ALU.add)
                yield
                t2 = norm(L, L["res"][:, :], L["x2"][:, :], [tr2])
                txb = f.pool([t2], pool.tensor_tensor, L["cx"][:, :], L["x2"][:, :], bdn_sb[:, :], ALU.add)
                yield
                t = f.pe([t2, teT], [tr(b3[:, k * P:(k + 1) * P], L["x2"][:, k * P:(k + 1) * P]) for k in range(KD)])
                t = f.act([t], act.copy, L["xT"][:, :, :].rearrange("p k t -> p (k t)"), b3[:, 0:D])
                yield
                tu = []
                for j in range(2):
                    tj = f.pe([t, th if j == 0 else tmu], [
                        mm(L["bank"][j][:, m * P:(m + 1) * P], wup[:, k, (4 * j + m) * P:(4 * j + m + 1) * P], L["xT"][:, k, :],
                           start=k == 0, stop=k == KD - 1) for m in range(4) for k in range(KD)])
                    tj = f.dve([tj], dve.tensor_tensor, L["up"][:, 4 * j:4 * j + 4, :],
                               L["bank"][j].rearrange("p (m t) -> p m t", m=4), spread(b128_sb[:, 1 + 4 * j:5 + 4 * j], P, 2), ALU.add)
                    tu.append(f.act([tj], act.activation, L["up"][:, 4 * j:4 * j + 4, :], L["up"][:, 4 * j:4 * j + 4, :], ACT.Relu,
                                    label=f"free{j}{n}"))
                    yield
                t = f.pe([tu[1], tr2], [mm(b2[:, 0:D], L["up"][:, m, :], wdn[:, m, :], start=m == 0, stop=m == FT - 1)
                                        for m in range(FT)])
                yield
                t = f.dve([t, txb], dve.tensor_tensor, L["res"][:, :], b2[:, 0:D], L["cx"][:, :], ALU.add, label=f"free2{n}")
                t = norm(L, L["res"][:, :], L["x3"][:, :], [t] + was("out"))
                f.dma([t], "act", f"out{n}", lambda i: x_all[:, bass.ds(LANES * i + n, 1), :], L["x3"][:, :].unsqueeze(1), label=f"out{n}")
                yield
                t = f.pe([t], [tr(b3[:, k * P:(k + 1) * P], L["x3"][:, k * P:(k + 1) * P]) for k in range(KD)])
                t = f.act([t] + was("outT"), act.copy, L["x3T"][:, :, :].rearrange("p k t -> p (k t)"), b3[:, 0:D], label=f"free3{n}")
                f.dma([t], "act", f"outT{n}", lambda i: xT_all[:, :, bass.ds((LANES * i + n) * P, P)], L["x3T"][:, :, :], label=f"outT{n}")

            f.lanes(*[sequence(L) for L in lanes], order="0100110001000101001010011111100011010110001110010101101011011001101010", split=31)
            f.play(NSEQ // LANES, join=[name for name in f.total if name != "table"], ahead=("sp",))
            c.close()

        layer0()


        gate_sb = sb("gate_sb", [P, KD, NE])
        first_slot = sb("first_slot", [P, NE])
        chosen_before = sb("chosen_before", [P, NE], BF16)
        slot_all = sb("slot_all", [P, NSEQ, NE])
        weight_all = sb("weight_all", [P, NSEQ, TOPK])

        tile_no = sb("tile_no", [P, 1])
        expert_no = sb("expert_no", [P, NE])
        upto = sb("upto", [NE, NE], BF16)
        index_all = sb("index_all", [P, NSEQ, TOPK], U32)
        tile_expert = sb("tile_expert", [1, NT + 2 * TPT], I32)
        tile_ids = sb("tile_ids", [P, NT + 2 * TPT], U32)
        count, tiles_of = sb("count", [NE, P]), sb("tiles_of", [NE, P])
        tiles_ofb = sb("tiles_ofb", [NE, P], BF16)
        base, end, mine = sb("base", [P, NE]), sb("end", [P, NE]), sb("mine", [P, NE])
        shift, hit, cols = sb("shift", [P, NE]), sb("hit", [P, 2, NE]), sb("cols", [P, 3])
        plan_i, line = sb("plan_i", [P, 1], I32), sb("line", [P, 1], U32)
        by_tile, by_tilef = sb("by_tile", [NT, PARTS, P], I32), sb("by_tilef", [NT, P])
        moved, is_in = sb("moved", [P, NSEQ, NE]), sb("is_in", [P, NSEQ, NE])
        best = sb("best", [P, NSEQ, TOPK])
        cross = ExitStack()

        def cross_lanes():
            def sb(name, shape, dt=F32):
                return cross.enter_context(nc.sbuf_tensor(name, shape, dt))

            lanes = []
            for n in range(LANES):
                s = lambda name, shape, dt=F32, n=n: sb(f"{name}c_{n}", shape, dt)
                lanes.append(dict(
                    n=n, bank=[ps[:, 4 * n + k, :] for k in range(4)], flat=ps[:, 4 * n:4 * n + 4, :],
                    x=s("x", [P, D]), ctx=s("ctx", [P, D]), kheads=s("kheads", [P, HX, D]),
                    vheads=s("vheads", [P, 2, HX * (P + HDX)]), soft=s("soft", [P, HX, D]),
                    pT=s("pT", [P, HX, D]), top=s("top", [P, HX]), rsum=s("rsum", [P, HX]),
                    res=s("res", [P, D]), x5=s("x5", [P, D]), x5T=s("x5T", [P, KD, P]),
                    prob=s("prob", [P, NE]), left=s("left", [P, NE]), slot=s("slot", [P, NE]),
                    chosen=s("chosen", [P, NE], BF16), best=s("best", [P, TOPK]), slots=s("slots", [P, TOPK]),
                    index=s("index", [P, TOPK], U32), weight=s("weight", [P, TOPK]), one=s("one", [P, 4]),
                    token=s("token", [P, 1], I32), zero=s("zero", [P, 1], I32), spare=s("spare", [P, 1], U32), junk=s("junk", [P, TOPK, NE]),
                    stats=s("stats", [P, 6]), mv=s("mv", [P, 4]), chain={}))
            return lanes

        cross_lane = cross_lanes()

        def scatter(after, part, lane, index, value, label=None):
            return f.step("pool", after, [(pool.indirect_dma_start, (
                id_parts[part], bass.IndirectOffsetOnAxis(ap=index, axis=0), value, None), {})], label, f"part{part}lane{lane}", apart=True)

        def first_scatters():
            lanes = cross_lane
            for L in lanes:
                t = f.pool([], pool.iota, L["token"][:, :], pattern=[[0, 1]], base=(L["n"] - LANES) * P, channel_multiplier=1)
                tz = f.pool([], pool.memset, L["zero"][:, :], 0)
                ti = f.pool([], pool.iota, L["spare"][:, :], pattern=[[0, 1]], base=TABLE - P, channel_multiplier=1)
                for k in range(PARTS):
                    first = scatter([tz, ti] + ([L["chain"][k]] if L["chain"] else []), k, L["n"], L["spare"][:, :], L["zero"][:, :])
                    for M in lanes[L["n"] + 1:]:
                        M["chain"][k] = first

        def cross_setup():
            lanes = cross_lane
            for L in lanes:
                f.pool([], pool.memset, L["vheads"][:, :, :], 0.0)
            f.dma([], "sp", "gate", gate_sb[:, :, :], gatew)
            f.pool([], pool.iota, first_slot[:, :], pattern=[[ROWS, NE]], base=1, channel_multiplier=0,
                   allow_small_or_imprecise_dtypes=True)
            f.pool([], pool.memset, chosen_before[:, :], 0.0)
            f.pool([], pool.affine_select, out=upto[:, :], in_=onesb[0:NE, 0:NE], compare_op=ALU.is_ge, fill=0.0,
                   base=0, pattern=[[1, NE]], channel_multiplier=-1)
            f.pool([], pool.iota, tile_no[:, :], pattern=[[0, 1]], base=0, channel_multiplier=1,
                   allow_small_or_imprecise_dtypes=True)
            f.pool([], pool.iota, expert_no[:, :], pattern=[[1, NE]], base=0, channel_multiplier=0,
                   allow_small_or_imprecise_dtypes=True)

        def attention1():
            c = ExitStack()

            def sb(name, shape, dt=F32):
                return c.enter_context(nc.sbuf_tensor(name, shape, dt))

            wh = sb("wh", [P, KD, 3, HD1])
            w_hi, w_lo = sb("w_hi", [P, KD, 3, HD1], F32R), sb("w_lo", [P, KD, 3, HD1], F32R)
            x_hi, x_lo = sb("x_hi", [P, KD, TOK], F32R), sb("x_lo", [P, KD, TOK], F32R)
            wo = sb("wo", [P, D])
            wo_hi, wo_lo = sb("wo_hi", [P, D], F32R), sb("wo_lo", [P, D], F32R)
            o_hi, o_lo = sb("o_hi", [P, TOK], F32R), sb("o_lo", [P, TOK], F32R)
            qT, kT = sb("qT1", [P, TOK]), sb("kT1", [P, TOK])
            vT, sums, oT = sb("vT1", [P, TOK]), sb("sums1", [P, TOK]), sb("oT1", [P, TOK])
            soft, rows = sb("soft1", [P, NSEQ, P]), sb("rows1", [P, NSEQ, P])
            top, rsum = sb("top1", [P, NSEQ]), sb("rsum1", [P, NSEQ])
            stats, mv = sb("stats1", [P, NSEQ, 6]), sb("mv1", [P, NSEQ, 2])
            var, rstd = sb("var1", [P, NSEQ]), sb("rstd1", [P, NSEQ])
            y = [ps[:, b // 2, (b % 2) * D:(b % 2 + 1) * D] for b in range(NSEQ)]
            sbank, abank = [ps[:, 4, :], ps[:, 5, :]], [ps[:, 6, :], ps[:, 7, :]]

            def load_qkv(after, head):
                return f.dma(after, "sp", "wh", wh[:, :, :, :], head)

            def split_weights(got):
                parts = []
                for which, name in enumerate("qkv"):
                    hi, lo = w_hi[:, :, which, :], w_lo[:, :, which, :]
                    t = f.act([got, Prev(f"{name} project1")] if got is not first_wh else [got], act.copy, hi, wh[:, :, which, :])
                    parts.append(f.pool([t], pool.tensor_tensor, lo, wh[:, :, which, :], hi, ALU.subtract, label="weights split"))
                return parts

            def project(which, got, read, free):
                name, dst = ("q", "k", "v")[which], (qT, kT, vT)[which]
                done = []
                for half in range(2):
                    cols = slice(half * 512, half * 512 + 512)
                    t = f.pe(got + free[half], [
                        mm(abank[half], w[:, k, which, :], x[:, k, cols], start=k == 0 and n == 0, stop=k == KD - 1 and n == 2)
                        for n, (w, x) in enumerate(((w_hi, x_hi), (w_hi, x_lo), (w_lo, x_hi))) for k in range(KD)],
                        label=f"{name} project{half}")
                    done.append(f.act([t] + read, act.copy, dst[:, cols], abank[half], label=f"{name}{half}") if half else
                                f.dve([t] + read, dve.tensor_copy, dst[:, cols], abank[half], label=f"{name}{half}"))
                return done

            def add_head(got_o, got_wo, sequences=range(NSEQ), stop=False):
                return f.pe([got_o, got_wo], [
                    mm(y[b], o[:, b * P:(b + 1) * P], w[:, :], start=False, stop=stop and b % 2 == 1 and n == 2)
                    for b in sequences for n, (o, w) in enumerate(((o_hi, wo_hi), (o_hi, wo_lo), (o_lo, wo_hi)))])

            def head(following):
                if following:
                    got = load_qkv([Prev("v project1")], lambda i: wqkv[i + 1, :, :, :, :])
                    got_wo = f.dma([Prev("wo split")], "sp", "wo", wo[:, :], lambda i: wo1[i, :, :])
                else:
                    got_wo = f.dma([Prev("wo split")], "sp", "wo", wo[:, :], wo1[H1 - 1, :, :])
                if following:
                    parts = split_weights(got)
                qk = [Prev(f"{name}{half}") for name in "qk" for half in range(2)]
                ts = []
                for half in range(2):
                    ts.append(f.pe(qk + [Prev(f"sums{half}")], [
                        mm(sbank[half][:, b * P:(b + 1) * P], qT[:, (4 * half + b) * P:(4 * half + b + 1) * P],
                           kT[:, (4 * half + b) * P:(4 * half + b + 1) * P]) for b in range(4)]))
                t_out = add_head(Prev("o split1"), Prev("wo split"))
                halves = [slice(0, 4), slice(4, 8)]
                te = []
                for half, hs in enumerate(halves):
                    s3 = sbank[half].rearrange("p (b t) -> p b t", b=4)
                    t = f.dve([ts[half]], dve.tensor_reduce, top[:, hs], s3, AX.X, ALU.max)
                    t = f.dve([t, Prev("column sums1")], dve.tensor_tensor, soft[:, hs, :], s3, spread(top[:, hs], P, 2), ALU.subtract)
                    te.append(f.act([t], act.activation, soft[:, hs, :], soft[:, hs, :], ACT.Exp, scale=HD1 ** -0.5))
                if following:
                    tq = project(0, [parts[0]], [ts[1]], [[Prev("v0")], [Prev("v1")]])
                t_rows = []
                for half, hs in enumerate(halves):
                    t = f.dve([te[half]], dve.tensor_reduce, rsum[:, hs], soft[:, hs, :], AX.X, ALU.add)
                    t = f.dve([t], dve.reciprocal, rsum[:, hs], rsum[:, hs])
                    t_rows.append(f.dve([t], dve.tensor_copy, rows[:, hs, :], spread(rsum[:, hs], P, 2)))
                if following:
                    tk = project(1, [parts[1]], [ts[1]], [[tq[0]], [tq[1]]])
                tsum = []
                for half in range(2):
                    t = f.pe([t_rows[half]], [mm(sbank[half][:, b * P:(b + 1) * P], rows[:, 4 * half + b, :], soft[:, 4 * half + b, :])
                                   for b in range(4)], label=f"column sums{half}")
                    t = f.act([t], act.copy, sums[:, 512 * half:512 * half + 512], sbank[half], label=f"sums{half}")
                    cols = slice(512 * half, 512 * half + 512)
                    tsum.append(f.dve([t, Prev(f"v{half}"), Prev("o split1")], dve.tensor_tensor, oT[:, cols], vT[:, cols],
                                      sums[:, cols], ALU.mult))
                    t = f.act([tsum[-1], t_out], act.copy, o_hi[:, cols], oT[:, cols])
                    f.dve([t], dve.tensor_tensor, o_lo[:, cols], oT[:, cols], o_hi[:, cols], ALU.subtract, label=f"o split{half}")
                t = f.act([got_wo, t_out], act.copy, wo_hi[:, :], wo[:, :])
                f.pool([t], pool.tensor_tensor, wo_lo[:, :], wo[:, :], wo_hi[:, :], ALU.subtract, label="wo split")
                if following:
                    project(2, [parts[2]], [tsum[1]], [[tk[0]], [tk[1]]])

            t = f.dve([], dve.memset, soft[:, 0:4, :], 0.0)
            zero = soft[:, 0:4, :].rearrange("p a b -> p (a b)")
            for part in (o_hi[:, 0:512], o_hi[:, 512:], o_lo[:, 0:512], o_lo[:, 512:], wo_hi[:, :], wo_lo[:, :]):
                f.dve([t], dve.tensor_copy, part, zero[:, 0:part.shape[1]])
            for k in range(4):
                f.pe([t], [mm(ps[:, k, :], soft[:, 0, :], soft[:, 0:4, :].rearrange("p a b -> p (a b)"), stop=False)])
            first_wh = load_qkv([], wqkv[0, :, :, :, :])
            t_x = []
            for half in range(2):
                cols = slice(half * 512, half * 512 + 512)
                t = f.act([], act.copy, x_hi[:, :, cols], xT_all[:, :, cols])
                t_x.append(f.dve([t], dve.tensor_tensor, x_lo[:, :, cols], xT_all[:, :, cols], x_hi[:, :, cols], ALU.subtract))
            parts = split_weights(first_wh)
            free = [[t_x[0]], [t_x[1]]]
            for which in range(3):
                free = [[t] for t in project(which, [parts[which]], [], free)]
            first_scatters()
            f.play()
            head(True)
            f.play(H1 - 1, join=("pe", "act", "dve", "wh"))
            head(False)
            cross_setup()
            for k in range(4):
                x = x_all[:, 2 * k:2 * k + 2, :].rearrange("p b d -> p (b d)")
                t = add_head(f.labels["o split1"], f.labels["wo split"], (2 * k, 2 * k + 1), stop=True)
                t = f.dve([t], dve.tensor_tensor, x, x, ps[:, k, :], ALU.add)
                for b in (2 * k, 2 * k + 1):
                    ts = f.dve([t], dve.bn_stats, stats[:, b, :], x_all[:, b, :])
            for b in range(NSEQ):
                t = f.dve([ts], dve.bn_aggr, mv[:, b, :], stats[:, b, :])
            t = f.dve([t], dve.tensor_scalar, var[:, :], mv[:, :, 1], EPS, None, ALU.add)
            tr_ = f.pool([t], pool.tensor_tensor, rstd[:, :], var[:, :], power[:, 0:NSEQ], ALU.pow)
            for b in range(NSEQ):
                f.dve([tr_], dve.tensor_scalar, x_all[:, b, :], x_all[:, b, :], mv[:, b, 0:1], rstd[:, b:b + 1],
                      ALU.subtract, ALU.mult)
            f.play(join=False)
            c.close()

        attention1()

        def cross1():
            x4_done = f.all_of("dve")

            def other(label, n):
                return Prev(f"{label}{n - 1}", turns=0) if n else Prev(f"{label}{LANES - 1}")

            def sequence(L):
                n, bank = L["n"], L["bank"]
                x, soft = L["x"], L["soft"]
                got_ctx = f.dma([Prev(f"kheads{n}"), Prev(f"ctxT{n}")], "sp", f"ctxc{n}", L["ctx"][:, :], lambda i: ctx_in[LANES * i + n, :, :])
                got_x = f.dma([Prev(f"residual{n}"), x4_done], "sp", f"xc{n}", L["x"][:, :].unsqueeze(1), lambda i: x_all[:, bass.ds(LANES * i + n, 1), :])
                tkh = f.pool([got_ctx, Prev(f"scores{n}")], pool.tensor_tensor, L["kheads"][:, :, :],
                             spread(L["ctx"][:, :], HX, 1), spread(headmask[:, :], D, 2), ALU.mult, label=f"kheads{n}")
                t = f.pe([got_ctx, Prev(f"free0{n}")], [tr(bank[0][:, k * P:(k + 1) * P], L["ctx"][:, k * P:(k + 1) * P]) for k in range(2)],
                         label=f"ctxT{n}")
                tv = f.dve([t, Prev(f"weighted{n}")], dve.tensor_copy,
                           L["vheads"][:, :, :].rearrange("p k (h s) -> p k h s", s=P + HDX)[:, :, :, 0:HDX],
                           bank[0][:, 0:D].rearrange("p (k h s) -> p k h s", k=2, h=HX))
                yield
                def scores(m, k, free):
                    return f.pe([got_x, tkh] + free, [mm(bank[k], x[:, m * P:(m + 1) * P],
                                                         L["kheads"][:, 2 * k:2 * k + 2, :].rearrange("p a b -> p (a b)"))],
                                label=f"scores{n}")

                ts = []
                for k in range(4):
                    ts.append(scores(0, k, [tv] if k == 0 else [Prev(f"free{k}{n}")]))
                    if k % 2:
                        yield
                for m in range(2):
                    halves = (0, 1) if m == 0 else (1, 0)
                    te, tn, tp = {}, {}, {}
                    for half in halves:
                        for k in (2 * half, 2 * half + 1) if m == 0 or half else (1, 0):
                            s3 = bank[k].rearrange("p (h t) -> p h t", h=2)
                            t = f.dve([ts[k]], dve.tensor_reduce, L["top"][:, 2 * k:2 * k + 2], s3, AX.X, ALU.max, negate=True)
                            for h in range(2):
                                te[half] = f.act([t, Prev(f"probT{n}")] if m == 0 else [t], act.activation, soft[:, 2 * k + h, :], s3[:, h, :],
                                                 ACT.Exp, bias=L["top"][:, 2 * k + h:2 * k + h + 1],
                                                 accum_out=L["rsum"][:, 2 * k + h:2 * k + h + 1])
                            yield
                    for half in halves:
                        hs = slice(4 * half, 4 * half + 4)
                        t = f.dve([te[half]], dve.reciprocal, L["rsum"][:, hs], L["rsum"][:, hs])
                        tn[half] = f.dve([t], dve.tensor_tensor, soft[:, hs, :], soft[:, hs, :], spread(L["rsum"][:, hs], D, 2), ALU.mult)
                        yield
                    for half in halves:
                        for k in (2 * half, 2 * half + 1):
                            t = f.pe([tn[half]], [tr(bank[k][:, (2 * h + u) * P:(2 * h + u + 1) * P], soft[:, 2 * k + h, u * P:(u + 1) * P])
                                                  for h in range(2) for u in range(2)], label=f"probT{n}")
                            dst = L["pT"][:, 2 * k:2 * k + 2, :].rearrange("p a b -> p (a b)")
                            tp[k] = f.act([t], act.copy, dst, bank[k]) if k % 2 else f.dve([t], dve.tensor_copy, dst, bank[k])
                            yield
                    if m == 0:
                        ts = {}
                        for k in (2, 3, 1):
                            ts[k] = scores(1, k, [tp[k]])
                            yield
                    t = f.pe([tp[0], tp[1], tp[2], tp[3], tv], [mm(bank[0][:, 0:P], L["vheads"][:, u, h * P:(h + 1) * P], L["pT"][:, h, u * P:(u + 1) * P],
                                                     start=h == 0 and u == 0, stop=h == HX - 1 and u == 1)
                                                  for h in range(HX) for u in range(2)], label=f"weighted{n}")
                    yield
                    t = f.dve([t], dve.tensor_tensor, L["res"][:, m * P:(m + 1) * P], bank[0][:, 0:P], x[:, m * P:(m + 1) * P],
                              ALU.add, label=f"residual{n}")
                    if m == 0:
                        ts[0] = scores(1, 0, [t])
                    yield
                t5 = norm(L, L["res"][:, :], L["x5"][:, :], [t, Prev(f"x5 out{n}")])
                f.dma([t5], "act", f"x5{n}", lambda i: x5_rows[bass.ds((LANES * i + n) * P, P), :], L["x5"][:, :], label=f"x5 out{n}")
                yield
                t = f.pe([t5, tp[1]], [tr(bank[1][:, k * P:(k + 1) * P], L["x5"][:, k * P:(k + 1) * P]) for k in range(KD)])
                t = f.act([t], act.copy, L["x5T"][:, :, :].rearrange("p k t -> p (k t)"), bank[1][:, 0:D], label=f"free1{n}")
                yield
                t = f.pe([t, tp[2]], [mm(bank[2][:, 0:NE], L["x5T"][:, k, :], gate_sb[:, k, :], start=k == 0, stop=k == KD - 1)
                                      for k in range(KD)])
                one = L["one"]
                t = f.dve([t], dve.tensor_reduce, one[:, 0:1], bank[2][:, 0:NE], AX.X, ALU.max, negate=True)
                t = f.act([t], act.activation, L["prob"][:, :], bank[2][:, 0:NE], ACT.Exp, bias=one[:, 0:1], accum_out=one[:, 1:2],
                          label=f"free2{n}")
                t = f.dve([t], dve.reciprocal, one[:, 2:3], one[:, 1:2])
                yield
                t = f.dve([t], dve.tensor_scalar, L["prob"][:, :], L["prob"][:, :], one[:, 2:3], None, ALU.mult)
                t = f.dve([t], dve.max, L["best"][:, :], L["prob"][:, :], apart=True)
                t = f.dve([t], dve.match_replace, L["left"][:, :], L["best"][:, :], L["prob"][:, :], -1.0, apart=True)
                yield
                tc = f.dve([t], dve.tensor_scalar, L["chosen"][:, :], L["left"][:, :], 0.0, None, ALU.is_lt)
                t = f.pe([tc, tp[3]] + [other("counted", n)], [
                    mm(bank[3][:, 0:NE], before[:, :], L["chosen"][:, :], stop=False),
                    mm(bank[3][:, 0:NE], onesb[:, :], chosen_before[:, :], start=False)])
                f.dve([t], dve.tensor_tensor, chosen_before[:, :], chosen_before[:, :], L["chosen"][:, :], ALU.add,
                                label=f"counted{n}")
                t = f.dve([t, Prev(f"slot out{n}")], dve.tensor_tensor, L["slot"][:, :], bank[3][:, 0:NE], first_slot[:, :], ALU.add, label=f"free3{n}")
                t = f.dve([t], dve.tensor_tensor, L["slot"][:, :], L["slot"][:, :], L["chosen"][:, :], ALU.mult)
                f.dma([t], "act", f"slot{n}", lambda i: slot_all[:, bass.ds(LANES * i + n, 1), :], L["slot"][:, :].unsqueeze(1), label=f"slot out{n}")
                yield
                chain = {}
                t = f.dve([t], dve.max, L["slots"][:, :], L["slot"][:, :], apart=True)
                ti = f.dve([t] + [Prev(f"scattered{k}lane{n}") for k in range(PARTS)], dve.tensor_scalar, L["index"][:, :], L["slots"][:, :], -1.0, None, ALU.add)
                tt = f.dve([], dve.tensor_scalar, L["token"][:, :], L["token"][:, :], float(LANES * P), None, ALU.add)
                for j in range(TOPK):
                    tw = f.dve([t, Prev(f"weight out{n}")], dve.scalar_tensor_tensor, out=L["junk"][:, j, :], in0=L["slot"][:, :], scalar=L["slots"][:, j:j + 1],
                               in1=L["prob"][:, :], op0=ALU.is_equal, op1=ALU.mult, accum_out=L["weight"][:, j:j + 1])
                f.dma([tw], "act", f"weight{n}", lambda i: weight_all[:, bass.ds(LANES * i + n, 1), :], L["weight"][:, :].unsqueeze(1), label=f"weight out{n}")
                f.dve([t], dve.tensor_copy, one[:, 3:4], one[:, 2:3], label=f"free0{n}")
                yield
                for j in range(TOPK):
                    k = j % PARTS
                    before_it = chain[k] if k in chain else other(f"scattered{k}lane", n)
                    chain[k] = scatter([ti, tt, before_it], k, n, L["index"][:, j:j + 1], L["token"][:, :], f"scattered{k}lane{n}")

            f.lanes(*[sequence(L) for L in cross_lane], order="11101100001111010010011000101000111000001001111000001110110011101011010011", split=19, last_after=4)
            f.play(NSEQ // LANES, ahead=("sp", "pool"))
            cross.close()

        cross1()

        def plan():
            t = f.pe([], [mm(ps[0:NE, 0, 0:P], chosen_before[:, :], onesb[:, :])])
            t = f.dve([t], dve.tensor_copy, count[:, :], ps[0:NE, 0, 0:P])
            t = f.dve([t], dve.tensor_scalar, tiles_of[:, :], count[:, :], 0.0, None, ALU.is_gt)
            for k in range(1, ROWS // P):
                t = f.dve([t], dve.scalar_tensor_tensor, out=tiles_of[:, :], in0=count[:, :], scalar=float(k * P), in1=tiles_of[:, :],
                          op0=ALU.is_gt, op1=ALU.add)
            t = f.dve([t], dve.tensor_copy, tiles_ofb[:, :], tiles_of[:, :])
            t = f.pe([t], [mm(ps[:, 1, 0:NE], tiles_ofb[:, :], before[0:NE, 0:NE]), mm(ps[:, 1, NE:2 * NE], tiles_ofb[:, :], upto[:, :])])
            t = f.dve([t], dve.tensor_copy, base[:, :], ps[:, 1, 0:NE])
            te = f.dve([], dve.tensor_copy, end[:, :], ps[:, 1, NE:2 * NE])
            t = f.dve([te], dve.tensor_tensor, mine[:, :], end[:, :], base[:, :], ALU.subtract)
            t = f.dve([t], dve.tensor_scalar, hit[:, 0, :], end[:, :], tile_no[:, 0:1], 0.0, ALU.is_le, ALU.add, accum_out=cols[:, 0:1])
            t2 = f.dve([], dve.scalar_tensor_tensor, out=hit[:, 1, :], in0=end[:, :], scalar=tile_no[:, 0:1], in1=mine[:, :],
                       op0=ALU.is_le, op1=ALU.mult, accum_out=cols[:, 1:2])
            t = f.dve([t2], dve.tensor_tensor, cols[:, 2:3], tile_no[:, :], cols[:, 1:2], ALU.subtract)
            t_line = f.dve([t], dve.scalar_tensor_tensor, out=line[:, :], in0=cols[:, 0:1], scalar=float(ROWS // P), in1=cols[:, 2:3],
                           op0=ALU.mult, op1=ALU.add)
            t = f.dve([t_line], dve.tensor_scalar, plan_i[:, :], cols[:, 0:1], float(NE - 1), None, ALU.min)
            t = f.dma([t], "sp", "plan", tile_expert_dram, plan_i[:, :])
            f.dve([], dve.memset, tile_expert[:, NT:], 0)
            f.dve([], dve.memset, tile_ids[:, NT:], 0)
            f.dma([t], "sp", "plan", tile_expert[:, 0:NT], tile_expert_dram.rearrange("t c -> (t c)").unsqueeze(0))
            t = f.dve([], dve.tensor_scalar, shift[:, :], base[:, :], float(P), float(LAG * P), ALU.mult, ALU.add)
            t = f.dve([t], dve.scalar_tensor_tensor, out=shift[:, :], in0=expert_no[:, :], scalar=-float(ROWS), in1=shift[:, :],
                      op0=ALU.mult, op1=ALU.add)
            t = f.dve([t], dve.tensor_tensor, moved[:, :, :], slot_all[:, :, :], spread(shift[:, :], NSEQ, 1), ALU.add)
            t = f.dve([t], dve.scalar_tensor_tensor, out=is_in[:, :, :], in0=slot_all[:, :, :], scalar=0.0, in1=moved[:, :, :],
                      op0=ALU.is_gt, op1=ALU.mult)
            for b in range(NSEQ):
                tb = f.dve([t], dve.max, best[:, b, :], is_in[:, b, :])
            f.dve([tb], dve.tensor_scalar, index_all[:, :, :], best[:, :, :], -1.0, None, ALU.add)
            for k in range(PARTS):
                t = f.step("pool", [t_line] + [f.all_of(f"part{k}lane{n}") for n in range(LANES)], [(pool.indirect_dma_start, (
                    by_tile[:, k, :], None, id_parts[k].rearrange("(l s) o -> l (s o)", s=P),
                    bass.IndirectOffsetOnAxis(ap=line[:, :], axis=0)), {})], None, "lines")
            t = f.dve([t], dve.tensor_tensor, by_tile[:, 0:2, :], by_tile[:, 0:2, :], by_tile[:, 2:4, :], ALU.add)
            t = f.dve([t], dve.tensor_tensor, by_tilef[:, :], by_tile[:, 0, :], by_tile[:, 1, :], ALU.add)
            t = f.pe([t], [tr(ps[:, 2, 0:NT], by_tilef[:, :])])
            f.dve([t], dve.tensor_copy, tile_ids[:, 0:NT], ps[:, 2, 0:NT])
            f.play(join=[name for name in f.total if not name.startswith("part")])

        plan()

        def experts():
            c = ExitStack()

            def sb(name, shape, dt=F32):
                return c.enter_context(nc.sbuf_tensor(name, shape, dt))

            tiles = []
            for u in range(TPT):
                s = lambda name, shape, dt=F32, u=u: sb(f"{name}_e{u}", shape, dt)
                tiles.append(dict(w=s("w", [P, WCOLS]), rows=s("rows", [P, D]), xT=s("xT", [P, KD, P]),
                                  gate=s("gate", [P, P]), h=s("h", [P, P]), o=s("o", [P, D]),
                                  t_bank=ps[:, u % 2, :], g_bank=ps[:, 2 + u % 2, :], o_bank=ps[:, 4 + u % 2, :]))
            half = TPT // 2
            ids = [sb(f"ids{k}", [P, half], U32) for k in range(2)]
            latest = f.latest
            experts_of_turn = []

            def read_experts(i):
                experts_of_turn[:] = read(tile_expert[0:1, bass.ds(TPT * i + TPT - LAG, TPT)])
                return tile_ids[:, bass.ds(TPT * i + TPT - LAG + half, half)]

            def read(ap):
                return nc.values_load_multi_w_load_instructions(
                    ap, engines=[mybir.EngineType.SP], min_val=0, max_val=NE - 1,
                    skip_runtime_bounds_check_because="the plan keeps them below the number of experts")[1]

            def ids_in(k, source):
                return f.dma([latest(f"got rows{(half * k + s - LAG) % TPT}") for s in range(half)], "sp", f"ids{k}", ids[k][:, :],
                             source, label=f"ids{k}")

            def fetch(s):
                u, (k, col) = (s - LAG) % TPT, divmod(s, half)
                f.dma([latest(f"down{u}")], "sp", f"w{u}", tiles[u]["w"][:, :],
                      lambda i: we[bass.ds(experts_of_turn[s], 1), :, :].rearrange("a p n -> (a p) n"), label=f"got w{u}")
                f.step("pool", [latest(f"ids{k}"), latest(f"turned{u}")], [(pool.indirect_dma_start, (
                    tiles[u]["rows"][:, :], None, x5_rows, bass.IndirectOffsetOnAxis(ap=ids[k][:, col:col + 1], axis=0)), {})],
                    f"got rows{u}", f"rows{u}", apart=True)

            def turn(u):
                T = tiles[u]
                t = f.pe([latest(f"got rows{u}"), latest(f"rowsT{(u - 2) % TPT}")], [
                    tr(T["t_bank"][:, k * P:(k + 1) * P], T["rows"][:, k * P:(k + 1) * P]) for k in range(KD)], label=f"turned{u}")
                f.act([t, latest(f"up{u}")], act.copy, T["xT"][:, :, :].rearrange("p k t -> p (k t)"), T["t_bank"][:, 0:D], label=f"rowsT{u}")

            def up(u):
                T = tiles[u]
                w13 = T["w"][:, 0:KD * 2 * INTER].rearrange("p (k n) -> p k n", k=KD)
                t = f.pe([latest(f"rowsT{u}"), latest(f"got w{u}"), latest(f"h{(u - 2) % TPT}")], [
                    mm(T["g_bank"][:, j * P:(j + 1) * P], w13[:, k, j * INTER:(j + 1) * INTER], T["xT"][:, k, :], start=k == 0, stop=k == KD - 1)
                    for j in range(2) for k in range(KD)], label=f"up{u}")
                t = f.act([t, latest(f"h{u}")], act.activation, T["gate"][:, :], T["g_bank"][:, 0:P], ACT.Silu)
                f.dve([t, latest(f"down{u}")], dve.tensor_tensor, T["h"][:, :], T["g_bank"][:, P:2 * P], T["gate"][:, :], ALU.mult, label=f"h{u}")

            def down(u, block):
                T = tiles[u]
                t = f.pe([latest(f"h{u}"), latest(f"o{(u - 2) % TPT}")], [
                    mm(T["o_bank"][:, 0:D], T["h"][:, :], T["w"][:, KD * 2 * INTER:])], label=f"down{u}")
                t = f.dve([t, latest(f"stored{u}")], dve.tensor_copy, T["o"][:, :], T["o_bank"][:, 0:D], label=f"o{u}")
                f.dma([t], "sp", f"stored{u}", lambda i: expert_rows[bass.ds(block(i) * P, P), :], T["o"][:, :], label=f"stored{u}")

            scattered = [f.all_of(f"part{k}lane{n}") for k in range(PARTS) for n in range(LANES)]
            for T in tiles[TPT - LAG:]:
                for name in ("w", "h"):
                    f.dve(scattered, dve.memset, T[name][:, :], 0.0)
                f.dve([], dve.memset, T["xT"][:, :, :], 0.0)
            nc.sync.wait_ge(f.sems["plan"], f.total["plan"])
            nc.sync.wait_ge(f.sems["dve"], f.total["dve"])
            first = read(tile_expert[0:1, 0:TPT - LAG])
            for u in range(TPT - LAG):
                f.dma(scattered, "sp", f"w{u}", tiles[u]["w"][:, :], we[bass.ds(first[u], 1), :, :].rearrange("a p n -> (a p) n"))
                f.step("pool", [f.all_of("dve")], [(pool.indirect_dma_start, (
                    tiles[u]["rows"][:, :], None, x5_rows, bass.IndirectOffsetOnAxis(ap=tile_ids[:, u:u + 1], axis=0)), {})],
                    None, f"rows{u}")
            f.dma([], "sp", "ids0", ids[0][:, :], tile_ids[:, TPT - LAG:TPT - LAG + half])
            act.preload_act_table(ACT.Silu)
            f.play(join=False)

            def tiles_of_turn(last):
                number = (lambda i: NT // TPT - 1) if last else (lambda i: i)
                ids_in(1, lambda i: read_experts(number(i)))
                for s in range(TPT):
                    turn(s)
                    up((s - 1) % TPT)
                    down((s - LAG) % TPT, lambda i, s=s: TPT * number(i) + s)
                    if s < LAG or not last:
                        fetch(s)
                    if s == half - 1 and not last:
                        ids_in(0, lambda i: tile_ids[:, bass.ds(TPT * i + 2 * TPT - LAG, half)])

            tiles_of_turn(False)
            f.play(NT // TPT - 1, join=("dve",))
            tiles_of_turn(True)
            up(TPT - 1)
            down(TPT - 2, lambda i: NT)
            down(TPT - 1, lambda i: NT + 1)
            f.play(join=False)
            c.close()

        ends = ExitStack()

        def combine_lanes():
            def sb(name, shape, dt=F32):
                return ends.enter_context(nc.sbuf_tensor(name, shape, dt))

            lanes = []
            for n in range(ENDS):
                s = lambda name, shape, dt=F32, n=n: sb(f"{name}o_{n}", shape, dt)
                lanes.append(dict(n=n, x5=s("x5", [P, D]), index=s("index", [P, TOPK], U32), weight=s("weight", [P, TOPK]),
                                  rows=s("rows", [P, TOPK, D]), acc=s("acc", [P, D]), y=s("y", [P, D]),
                                  stats=s("stats", [P, 6]), mv=s("mv", [P, 4])))
            return lanes

        combine_lane = combine_lanes()

        experts()

        def combine():
            written = [f.all_of(f"stored{u}") for u in range(TPT)]

            def sequence(L):
                n = L["n"]
                seq = lambda src: (lambda i: src[:, bass.ds(ENDS * i + n, 1), :])
                summed = Prev(f"summed{n}")
                ti = f.dma([Prev(f"gathered{n}")], "sp", f"oi{n}", L["index"][:, :].unsqueeze(1), seq(index_all))
                f.dma([summed], "sp", f"ox{n}", L["x5"][:, :], lambda i: x5_rows[bass.ds((ENDS * i + n) * P, P), :])
                tx = f.dma([summed], "sp", f"ox{n}", L["weight"][:, :].unsqueeze(1), seq(weight_all))
                got = []
                for j in range(TOPK):
                    got.append(f.step("pool", [ti, summed] + written, [(pool.indirect_dma_start, (
                        L["rows"][:, j, :], None, expert_rows, bass.IndirectOffsetOnAxis(ap=L["index"][:, j:j + 1], axis=0)), {})],
                        f"gathered{n}", f"or{n}" if j < TOPK - 1 else f"last or{n}", apart=True))
                yield
                t = tx
                for j in range(TOPK):
                    src = L["x5"] if j == 0 else L["acc"]
                    t = f.dve([t, got[max(j, TOPK - 2)]], dve.scalar_tensor_tensor, out=L["acc"][:, :], in0=L["rows"][:, j, :],
                              scalar=L["weight"][:, j:j + 1], in1=src[:, :], op0=ALU.mult, op1=ALU.add, label=f"summed{n}")
                yield
                t = norm(L, L["acc"][:, :], L["y"][:, :], [t, Prev(f"y out{n}")])
                f.dma([t], "act", f"y{n}", lambda i: out[bass.ds(ENDS * i + n, 1), :, :].rearrange("a p d -> (a p) d"), L["y"][:, :], label=f"y out{n}")

            f.lanes(*[sequence(L) for L in combine_lane], order="011100", split=1)
            f.play(NSEQ // ENDS, join=False)
            f.join()

        combine()
        ends.close()


def layout(x, ctx_2048, L0_attn_Wq, L0_attn_Wk, L0_attn_Wv, L0_attn_Wo, L0_xattn_theta_w, L0_xattn_theta_b,
           L0_xattn_phi_w, L0_xattn_phi_b, L0_xattn_g_w, L0_xattn_g_b, L0_xattn_ln_gamma, L0_xattn_ln_beta,
           L0_xattn_out_w, L0_xattn_out_b, L0_ffn_w_up_q, L0_ffn_w_up_scale, L0_ffn_b_up, L0_ffn_w_up_lora_a,
           L0_ffn_w_up_lora_b, L0_ffn_w_down_q, L0_ffn_w_down_scale, L0_ffn_b_down, L0_ffn_w_down_lora_a,
           L0_ffn_w_down_lora_b, L1_attn_w_qkv, L1_attn_w_o, L1_ffn_gate_w, L1_ffn_w13, L1_ffn_w2):
    def rows(w):
        return w.reshape(-1, P, w.shape[-1]).transpose(1, 0, 2)

    qkv = L1_attn_w_qkv.reshape(KD, P, 3, H1, HD1).transpose(3, 1, 0, 2, 4)
    w13 = L1_ffn_w13.transpose(0, 2, 1).reshape(NE, KD, P, 2 * INTER).transpose(0, 2, 1, 3).reshape(NE, P, -1)
    w2 = L1_ffn_w2.transpose(0, 2, 1)
    arrays = dict(
        x_in=x, ctx_in=ctx_2048,
        w0=np.stack([rows(w.T) for w in (L0_attn_Wq, L0_attn_Wk, L0_attn_Wv, L0_attn_Wo)], 1),
        thw=np.stack([w.T for w in (L0_xattn_theta_w, L0_xattn_phi_w, L0_xattn_g_w)], 1),
        outw=L0_xattn_out_w.T,
        bias64=np.stack([L0_xattn_theta_b, L0_xattn_phi_b], 1),
        bias128=np.concatenate([L0_xattn_out_b[:, None], L0_ffn_b_up.reshape(FT, P).T], 1),
        gb=L0_xattn_g_b[None], gamma=L0_xattn_ln_gamma, beta=L0_xattn_ln_beta,
        upq=rows(L0_ffn_w_up_q.T), ups=L0_ffn_w_up_scale.T,
        upa=L0_ffn_w_up_lora_a.T, upb=L0_ffn_w_up_lora_b,
        dnq=rows(L0_ffn_w_down_q.T), dns=L0_ffn_w_down_scale.T, bdn=L0_ffn_b_down[None],
        dna=L0_ffn_w_down_lora_a.T, dnb=L0_ffn_w_down_lora_b,
        wqkv=qkv, wo1=L1_attn_w_o.reshape(H1, P, D), gatew=rows(L1_ffn_gate_w.T),
        we=np.concatenate([w13, w2], 2))
    return {n: np.ascontiguousarray(a) for n, a in arrays.items()}


def kernel(**inputs):
    import concourse.bacc as bacc
    from concourse.bass_utils import run_bass_kernel_spmd

    nc = bacc.Bacc("TRN2", target_bir_lowering=False, num_devices=1)
    arrays = {f"in_{name}": a for name, a in layout(**{k: np.asarray(v) for k, v in inputs.items()}).items()}
    args = [nc.dram_tensor(name, a.shape, mybir.dt.from_np(a.dtype), kind="ExternalInput").ap() for name, a in arrays.items()]
    out = nc.dram_tensor("out", (NSEQ, P, D), F32, kind="ExternalOutput").ap()
    decoder(nc, *args, out)
    result = run_bass_kernel_spmd(nc, [arrays], core_ids=[0])
    return result.results[0]["out"]
```
